# Optimizing a Trainium2 kernel written in Bass

```python
import numpy as np
import jax
import jax.numpy as jnp

def _softmax(x, axis=-1):
    return jax.nn.softmax(x, axis=axis)

def _gelu(x):
    return jax.nn.gelu(x, approximate=True)

def _silu(x):
    return jax.nn.silu(x)

def _sigmoid(x):
    return jax.nn.sigmoid(x)

def _layernorm(x, axis=-1, eps=1e-05):
    m = jnp.mean(x, axis=axis, keepdims=True)
    v = jnp.var(x, axis=axis, keepdims=True)
    return (x - m) / jnp.sqrt(v + eps)

def _scatter_add(tgt, idx, src, axis=0):
    return tgt.at[idx].add(src)

def _segment_sum(src, seg, n):
    return jax.ops.segment_sum(src, seg, n)
kernel_name = 'mk_macaron_d1_jaxref_r8_aea259'

def setup_inputs(seed: int=0):
    np.random.seed(seed)
    _w = jnp.asarray

    def _L0_attn_setup():
        import jax, jax.numpy as jnp
        import numpy as np
        NUM_HEADS = 16
        key = jax.random.key(seed)
        ks = jax.random.split(key, 11)
        B, S, D = (4, 128, 128)
        M = 128
        hd = D // NUM_HEADS
        s = 0.02
        return {'x': jax.random.normal(ks[0], (B, S, D), jnp.float32), 'Wq': jax.random.normal(ks[1], (D, D), jnp.float32) * s, 'bq': jax.random.normal(ks[2], (D,), jnp.float32) * s, 'Wk': jax.random.normal(ks[3], (D, D), jnp.float32) * s, 'bk': jax.random.normal(ks[4], (D,), jnp.float32) * s, 'Wv': jax.random.normal(ks[5], (D, D), jnp.float32) * s, 'bv': jax.random.normal(ks[6], (D,), jnp.float32) * s, 'Wo': jax.random.normal(ks[7], (D, D), jnp.float32) * s, 'bo': jax.random.normal(ks[8], (D,), jnp.float32) * s, 'rel_k': jax.random.normal(ks[9], (2 * M + 1, hd), jnp.float32), 'rel_v': jax.random.normal(ks[10], (2 * M + 1, hd), jnp.float32)}
    _L0_attn_in = _L0_attn_setup()

    def _L0_ffn_setup():
        import jax, jax.numpy as jnp
        import numpy as np
        HIDDEN = 128
        INTER = 512
        key = jax.random.key(seed)
        k1, k2, k3, k4, k5 = jax.random.split(key, 5)
        hidden_states = jax.random.normal(k1, (4, 256, HIDDEN), dtype=jnp.float32)
        W1 = jax.random.normal(k2, (HIDDEN, INTER), dtype=jnp.float32) * (1.0 / np.sqrt(HIDDEN))
        b1 = jax.random.normal(k3, (INTER,), dtype=jnp.float32) * 0.02
        W2 = jax.random.normal(k4, (INTER, HIDDEN), dtype=jnp.float32) * (1.0 / np.sqrt(INTER))
        b2 = jax.random.normal(k5, (HIDDEN,), dtype=jnp.float32) * 0.02
        return {'hidden_states': hidden_states, 'W1': W1, 'b1': b1, 'W2': W2, 'b2': b2}
    _L0_ffn_in = _L0_ffn_setup()
    _d = {'L0_attn_x': _L0_attn_in['x'], 'L0_attn_Wq': _L0_attn_in['Wq'], 'L0_attn_bq': _L0_attn_in['bq'], 'L0_attn_Wk': _L0_attn_in['Wk'], 'L0_attn_bk': _L0_attn_in['bk'], 'L0_attn_Wv': _L0_attn_in['Wv'], 'L0_attn_bv': _L0_attn_in['bv'], 'L0_attn_Wo': _L0_attn_in['Wo'], 'L0_attn_bo': _L0_attn_in['bo'], 'L0_attn_rel_k': _L0_attn_in['rel_k'], 'L0_attn_rel_v': _L0_attn_in['rel_v'], 'L0_ffn_W1': _L0_ffn_in['W1'], 'L0_ffn_b1': _L0_ffn_in['b1'], 'L0_ffn_W2': _L0_ffn_in['W2'], 'L0_ffn_b2': _L0_ffn_in['b2']}
    _x0 = _d['L0_attn_x']
    _d['L0_attn_x'] = jax.random.normal(jax.random.fold_in(jax.random.key(seed), 1), (8, 512, 128), dtype=_x0.dtype)
    del _x0
    return _d

def reference(L0_attn_x, L0_attn_Wq, L0_attn_bq, L0_attn_Wk, L0_attn_bk, L0_attn_Wv, L0_attn_bv, L0_attn_Wo, L0_attn_bo, L0_attn_rel_k, L0_attn_rel_v, L0_ffn_W1, L0_ffn_b1, L0_ffn_W2, L0_ffn_b2):

    def _L0_attn_ref(x, Wq, bq, Wk, bk, Wv, bv, Wo, bo, rel_k, rel_v):
        import jax, jax.numpy as jnp
        import numpy as np
        NUM_HEADS = 16
        B, S, D = x.shape
        H = NUM_HEADS
        hd = D // H
        M = (rel_k.shape[0] - 1) // 2

        def proj(W, b):
            return (x @ W.T + b).reshape(B, S, H, hd).transpose(0, 2, 1, 3)
        q = proj(Wq, bq)
        k = proj(Wk, bk)
        v = proj(Wv, bv)
        r = jnp.arange(S)
        idx = jnp.clip(r[None, :] - r[:, None], -M, M) + M
        rpk = rel_k[idx]
        rpv = rel_v[idx]
        content = jnp.einsum('bhqd,bhkd->bhqk', q, k)
        relative = jnp.einsum('bhqd,qkd->bhqk', q, rpk)
        scores = (content + relative) / jnp.sqrt(jnp.float32(hd))
        w = jax.nn.softmax(scores, axis=-1)
        out = jnp.einsum('bhqk,bhkd->bhqd', w, v) + jnp.einsum('bhqk,qkd->bhqd', w, rpv)
        out = out.transpose(0, 2, 1, 3).reshape(B, S, D)
        return out @ Wo.T + bo

    def _L0_ffn_ref(hidden_states, W1, b1, W2, b2):
        import jax, jax.numpy as jnp
        import numpy as np
        HIDDEN = 128
        INTER = 512
        h = jax.nn.relu(jnp.einsum('bsh,hi->bsi', hidden_states, W1) + b1)
        return jnp.einsum('bsi,ih->bsh', h, W2) + b2
    x = L0_attn_x
    x = x + 0.5 * _L0_ffn_ref(_layernorm(x, axis=-1), L0_ffn_W1, L0_ffn_b1, L0_ffn_W2, L0_ffn_b2)
    x = x + _L0_attn_ref(_layernorm(x, axis=-1), L0_attn_Wq, L0_attn_bq, L0_attn_Wk, L0_attn_bk, L0_attn_Wv, L0_attn_bv, L0_attn_Wo, L0_attn_bo, L0_attn_rel_k, L0_attn_rel_v)
    x = x + 0.5 * _L0_ffn_ref(_layernorm(x, axis=-1), L0_ffn_W1, L0_ffn_b1, L0_ffn_W2, L0_ffn_b2)
    return x

_drawn_inputs = setup_inputs


def setup_inputs(seed=0):
    import zlib

    import numpy as np

    out = dict(_drawn_inputs(seed))
    spreads = {}
    factors = {'L0_attn_Wq': 6.465,
     'L0_attn_bq': 8.0,
     'L0_attn_Wk': 8.0,
     'L0_attn_bk': 8.0,
     'L0_attn_Wv': 7.096,
     'L0_attn_bv': 8.0,
     'L0_attn_bo': 3.181,
     'L0_attn_rel_k': 5.117,
     'L0_ffn_b1': 5.104,
     'L0_ffn_b2': 3.433}
    for name, (base, spread) in spreads.items():
        noise = np.random.default_rng([zlib.crc32(name.encode()), seed]).standard_normal(out[name].shape)
        drawn = base * np.exp(spread * noise) if base else spread * noise
        out[name] = jnp.asarray(drawn.astype(out[name].dtype))
    for name, factor in factors.items():
        out[name] = (out[name] * factor).astype(out[name].dtype)
    return out
```

```python
from contextlib import ExitStack

import numpy as np

import concourse.bass as bass
from concourse import mybir

F32 = mybir.dt.float32
BF16 = mybir.dt.bfloat16
ALU = mybir.AluOpType
ACT = mybir.ActivationFunctionType
AX = mybir.AxisListType
RMAX = bass.bass_isa.ReduceOp.max

P = 128
B, S, D = 8, 512, 128
H, HD = 16, 8
INTER = 512
REL = 128
NC = S // P
UQ = 32
UPG = P // UQ
UPB = S // UQ
COLS = H * UQ
EPS = 1e-5
SCALE = float(HD) ** -0.5

PAIRS = [(0, 0), (0, 1), (1, 0), (1, 1), (0, 2), (2, 0), (1, 2), (2, 1)]
NP = len(PAIRS)
HALF = NP * HD

TR0, TRW = 512, 1024
TV0 = 2 * P - 1
TVW = 3 * P
OCT = 8
NO = P // OCT

NSTAGE = 4 * NC + 3
KEYS, QUERIES, VALUES = 4 * NC, 4 * NC + 1, 4 * NC + 2


def by_act(k):
    return sum(1 for s in range(k + 1) if s < 4 * NC and s % 4 != 2 or s in (KEYS, QUERIES))


ACT_STAGES = by_act(NSTAGE - 1)


def stages_at(t):
    if t < 2:
        return [[], [0]][t], [[], [1]][t]
    return [k for k in (2 * t - 3,) if 2 < k < NSTAGE], [k for k in (2 * t - 2,) if k < NSTAGE]


NORMS = NC + 1
K_SLOT = KEYS // 2 + 2
Q_SLOT = K_SLOT
V_RAW_SLOT = VALUES // 2 + 2
V_SLOT = 2
TAIL = 12


def constants():
    p = np.arange(P)
    ident = np.eye(P, dtype=np.float32)
    ones = np.zeros((P, 4, 32), np.float32)
    for hh in range(4):
        ones[:, hh, 8 * hh:8 * hh + 8] = 1
    sel = np.zeros((P, 4, 32), np.float32)
    for hh in range(4):
        sel[p, hh, 8 * hh + p % 8] = 1
    own = np.zeros((P, 2, OCT), np.float32)
    own[p, p // 64, 7 - (p % 64) // 8] = 1
    part = np.zeros((P, 3), np.float32)
    part[p, [PAIRS[(r % HALF) // HD][1] for r in p]] = 1
    return np.ascontiguousarray(np.concatenate(
        [ident, ones.reshape(P, -1), sel.reshape(P, -1), own.reshape(P, -1), part], axis=1))


CW = constants().shape[1]
ZEROED = 7


def build(nc, x, wqT, wkT, wvT, woT, bq, bk, bv, bo, relkT, relv, w1, b1, w2, b2, cst, out):
    with ExitStack() as ctx:
        def sb(name, shape, dt=F32):
            return ctx.enter_context(nc.sbuf_tensor(name, shape, dt))

        def ps(name, shape):
            return ctx.enter_context(nc.psum_tensor(name, shape, F32))

        def sem(name):
            return ctx.enter_context(nc.semaphore(name))

        stack_k = nc.dram_tensor("stack_k", (2, H, NP, HD, S), BF16).ap()
        stack_q = nc.dram_tensor("stack_q", (2, H, NP, HD, S), BF16).ap()
        stack_qe = nc.dram_tensor("stack_qe", (2, H, NP, HD, S), BF16).ap()
        stack_qo = nc.dram_tensor("stack_qo", (2, H, NP, HD, S), BF16).ap()
        relv_ext = nc.dram_tensor("relv_ext", (2 * TV0 + 1, HD), F32).ap()

        w1_sb = sb("w1_sb", [P, INTER])
        w2_sb = sb("w2_sb", [P, NC, D])
        wq_sb, wk_sb, wv_sb, wo_sb = (sb(n, [P, D]) for n in ("wq_sb", "wk_sb", "wv_sb", "wo_sb"))
        b1_sb = sb("b1_sb", [P, NC])
        bq_sb, bk_sb = sb("bq_sb", [P, 1]), sb("bk_sb", [P, 1])
        bv_sb, bo_sb, b2_sb = sb("bv_sb", [P, D]), sb("bo_sb", [P, D]), sb("b2_sb", [P, D])
        b2_half = sb("b2_half", [P, D])
        relv_far = sb("relv_far", [P, 2, HD])
        cst_sb = sb("cst_sb", [P, CW])
        ident = cst_sb[:, 0:P]
        ones = cst_sb[:, P:2 * P].rearrange("p (a b) -> p a b", a=4)
        sel = cst_sb[:, 2 * P:3 * P].rearrange("p (a b) -> p a b", a=4)
        own = cst_sb[:, 3 * P:3 * P + 2 * OCT].rearrange("p (a b) -> p a b", a=2)
        part = cst_sb[:, 3 * P + 2 * OCT:CW]
        tr = sb("tr", [P, TRW], BF16)
        tv = sb("tv", [P, TVW * HD])

        x_in = sb("x_in", [P, NC, D])
        x1 = [sb(f"x1_{i}", [P, NC, D]) for i in range(2)]
        xn1, xn2, xn3 = sb("xn1", [P, D]), sb("xn2", [P, D]), sb("xn3", [P, D])
        st = sb("st", [P, 3, 6])
        mv = sb("mv", [P, 3, 2])
        var = sb("var", [P, 3])
        rstd = sb("rstd", [P, 3])
        minus_half = sb("minus_half", [P, 2])
        xn1T, xn3T = sb("xn1T", [P, P]), sb("xn3T", [P, P])
        xn2T = sb("xn2T", [P, S])
        hT, h3T = sb("hT", [P, NC, P]), sb("h3T", [P, NC, P])
        xh = sb("xh", [P, D])
        xa = sb("xa", [P, D])
        x2 = [sb(f"x2_{i}", [P, D]) for i in range(2)]
        xf = sb("xf", [P, D])
        out_sb = [sb(f"out_sb{i}", [P, D]) for i in range(2)]

        qf, kf = sb("qf", [P, S]), sb("kf", [P, S])
        qp, kp = sb("qp", [P, 3, S], BF16), sb("kp", [P, 3, S], BF16)
        qe, qo = sb("qe", [P, 3, S], BF16), sb("qo", [P, 3, S], BF16)
        k2 = [sb(f"k2_{i}", [P, H // 2, S], BF16) for i in range(2)]
        qh = sb("qh", [P, NC, H, P], BF16)
        qq = sb("qq", [P, NC, H, P], BF16)
        v_raw, v_sum = sb("v_raw", [P, NC, D]), sb("v_sum", [P, NC, D])
        v_pad = sb("v_pad", [P, NC, H, 32])
        v_far = sb("v_far", [P, NC, H, 32])

        w = [sb(f"weights{i}", [P, NC, H, P]) for i in range(2)]
        mtmp = sb("mtmp", [P, 2, H, UQ])
        mx, mall = sb("mx", [P, COLS]), sb("mall", [P, COLS])
        rown = sb("rown", [P, H, P])
        trf = rown[:, 0:TRW // P, :].rearrange("p a b -> p (a b)")
        trr = rown[:, TRW // P:2 * TRW // P, :].rearrange("p a b -> p (a b)")
        trp = mtmp[:, 0].rearrange("p h q -> p (h q)").bitcast(BF16)
        rden = sb("rden", [P, P])
        attT = sb("attT", [P, P])

        ps_s = ps("ps_s", [P, NC * COLS])
        ps_r = ps("ps_r", [P, 512])
        ps_o = ps("ps_o", [P, 512])
        ps_a = ps("ps_a", [P, 512])
        ps_b = ps("ps_b", [P, 512])

        c_loaded = sem("c_loaded")
        ext_made = sem("ext_made")
        zeroed = sem("zeroed")
        half_made = sem("half_made")
        tr_step = sem("tr_step")
        x_loaded = sem("x_loaded")
        stats = [sem(f"stats{i}") for i in range(3)]
        var_made = [sem("var_made_pre"), sem("var_made_post")]
        rstd_made = [sem("rstd_made_pre"), sem("rstd_made_post")]
        xn_made = [sem(f"xn_made{i}") for i in range(3)]
        pre_mm = sem("pre_mm")
        pre_act = sem("pre_act")
        x1_made = sem("x1_made")
        q_split, k_split = sem("q_split"), sem("k_split")
        qeo_made = sem("qeo_made")
        v_made = sem("v_made")
        v_sums, v_laid = sem("v_sums"), sem("v_laid")
        k_stored, q_stored = sem("k_stored"), sem("q_stored")
        k_ready = sem("k_ready")
        q_ready = [sem(f"q_ready{g}") for g in range(NC)]
        scored = sem("scored")
        evacuated = sem("evacuated")
        mtmp_made, maxed = sem("mtmp_made"), sem("maxed")
        max_known = sem("max_known")
        shifted = sem("shifted")
        exped = sem("exped")
        v_used = sem("v_used")
        rel_done = sem("rel_done")
        masked = sem("masked")
        o_done = sem("o_done")
        rden_made, att_made = sem("rden_made"), sem("att_made")
        post_mm = sem("post_mm")
        x2_made = sem("x2_made")
        xn3T_made, h3_made = sem("xn3T_made"), sem("h3_made")
        xf_made, fin_made = sem("xf_made"), sem("fin_made")
        wait_held = sem("wait_held")
        out_stored = [sem(f"out_stored{i}") for i in range(2)]

        x_t = x.rearrange("b (t p) d -> b p t d", p=P)
        out_t = out.rearrange("b (t p) d -> b t p d", p=P)
        loads = [
            (w1_sb[:], w1), (w2_sb[:], w2.rearrange("(c p) d -> p c d", p=P)),
            (wq_sb[:], wqT), (wk_sb[:], wkT), (wv_sb[:], wvT), (wo_sb[:], woT),
            (b1_sb[:], b1), (bq_sb[:], bq), (bk_sb[:], bk),
            (bv_sb[:], bv), (bo_sb[:], bo), (b2_sb[:], b2), (cst_sb[:], cst),
        ]
        NEARW = 2 * REL + 1
        for r in range(P // HD):
            j0 = TR0 - REL + (r * HD) // HALF
            loads.append((trf[HD * r:HD * r + HD, j0:j0 + NEARW], relkT))
        far_rows = [relv[0:1, :], relv[2 * REL:2 * REL + 1, :]]
        N_LOADS = len(loads) + 3

        block = ctx.enter_context(nc.Block())

        def every_batch(e, body, tail):
            body(0, 0, True)
            with e.Fori(0, (B - 2) // 2) as n:
                body(2 * n + 1, 1, True)
                body(2 * n + 2, 0, True)
            body(B - 1, 1, False)
            tail(B - 1)

        def at_least(e, s, n):
            if not isinstance(n, int) or n > 0:
                e.wait_ge(s, n)

        def stands_alone(e):
            e.sem_inc(wait_held, 1)

        def live(G):
            return not isinstance(G, int) or 0 <= G < B * NC

        @block.sync
        def _(sp):
            sp.dma_start(x_in[:], x_t[0]).then_inc(x_loaded, 16)
            mid = TV0 - REL
            sp.dma_start(relv_ext[mid:mid + NEARW, :], relv).then_inc(ext_made, 16)
            sp.dma_start(relv_ext[0:mid, :], bass.AP(relv.tensor, 0, [[0, mid], [1, HD]])).then_inc(ext_made, 16)
            sp.dma_start(relv_ext[mid + NEARW:, :],
                         bass.AP(relv.tensor, 2 * REL * HD, [[0, mid], [1, HD]])).then_inc(ext_made, 16)
            for dst, src in loads:
                sp.dma_start(dst, src).then_inc(c_loaded, 16)
            for n in range(2):
                sp.dma_start(relv_far[:, n, :],
                             bass.AP(relv.tensor, n * 2 * REL * HD, [[0, P], [1, HD]])).then_inc(c_loaded, 16)
            sp.wait_ge(ext_made, 48)
            sp.dma_start(tv[:], bass.AP(relv_ext.tensor, 0, [[HD, P], [1, TVW * HD]])).then_inc(c_loaded, 16)

            def store_stacks(b, par):
                at_least(sp, k_split, 4 * b + 4)
                for c in range(NP):
                    sp.dma_start(stack_k[par].rearrange("h c d s -> c h d s")[c],
                                 kp[:, PAIRS[c][1], :]).then_inc(k_stored, 16)
                at_least(sp, qeo_made, b + 1)
                for c in range(NP):
                    for dst, src in ((stack_q, qp), (stack_qe, qe), (stack_qo, qo)):
                        sp.dma_start(dst[par].rearrange("h c d s -> c h d s")[c],
                                     src[:, PAIRS[c][0], :]).then_inc(q_stored, 16)
                sp.wait_ge(k_stored, 16 * NP * (b + 1))
                for hp in range(2):
                    sp.dma_start(k2[par][HALF * hp:HALF * hp + HALF],
                                 stack_k[par].rearrange("(a hp) c d s -> hp (c d) a s", hp=2)[hp]).then_inc(k_ready, 16)
                sp.wait_ge(q_stored, 48 * NP * (b + 1))

            def load_queries(b, par, g):
                at_least(sp, scored, 4 * (UPB * (b - 1) + UPG * (g + 1)))
                q = slice(P * g, P * g + P)
                for hp in range(2):
                    rows = slice(HALF * hp, HALF * hp + HALF)
                    sp.dma_start(qh[rows, g].rearrange("r (a hp) q -> r hp a q", hp=2)[:, hp],
                                 stack_q[par].rearrange("(a hp) c d s -> hp (c d) a s", hp=2)[hp][:, :, q]
                                 ).then_inc(q_ready[g], 16)
                    sp.dma_start(qq[rows, g],
                                 (stack_qe, stack_qo)[hp][par].rearrange("h c d s -> (c d) h s")[:, :, q]
                                 ).then_inc(q_ready[g], 16)

            def store_out(b, back):
                G = NC * b - back
                if not live(G):
                    return
                at_least(sp, fin_made, G + 1)
                stands_alone(sp)
                bb, g = b - (back + NC - 1) // NC, (-back) % NC
                sp.dma_start(out_t[bb, g], out_sb[g % 2][:]).then_inc(out_stored[g % 2], 16)

            sp.wait_ge(zeroed, ZEROED)
            store_stacks(0, 0)
            for g in range(NC):
                load_queries(0, 0, g)

            def body(b, par, more):
                if more:
                    at_least(sp, x1_made, 2 * NC * (b + 1))
                    stands_alone(sp)
                    sp.dma_start(x_in[:], x_t[b + 1]).then_inc(x_loaded, 16)
                for back in (3, 2, 1):
                    store_out(b, back)
                if more:
                    store_stacks(b + 1, 1 - par)
                    for g in range(NC - 1):
                        load_queries(b + 1, 1 - par, g)
                store_out(b, 0)
                if more:
                    load_queries(b + 1, 1 - par, NC - 1)

            def tail(b):
                for back in (-1, -2, -3):
                    store_out(b, back)
                for i in range(2):
                    sp.wait_ge(out_stored[i], 16 * B * NC // 2)

            every_batch(sp, body, tail)

        @block.tensor
        def _(pe):
            def stage(b, k):
                n = NSTAGE * b + k
                j, part_k = divmod(k, 4)
                if k == 0:
                    at_least(pe, v_made, b)
                elif k < 4 * NC and part_k == 3:
                    at_least(pe, xn_made[1], NC * b + j + 1)
                elif k - 1 < 4 * NC and (k - 1) % 4 == 2:
                    pass
                else:
                    at_least(pe, pre_act, ACT_STAGES * b + by_act(k - 1))
                if k >= 4 * NC:
                    if k == VALUES:
                        for c in range(NC):
                            mm = pe.matmul(ps_a[:, P * c:P * c + P], xn2T[:, P * c:P * c + P], wv_sb[:],
                                           start=True, stop=True)
                    else:
                        mm = pe.matmul(ps_a[:], (wk_sb if k == KEYS else wq_sb)[:], xn2T[:], start=True, stop=True)
                elif part_k == 0:
                    at_least(pe, xn_made[0], NC * b + j + 1)
                    mm = pe.transpose(ps_a[:, 0:P], xn1[:], ident)
                elif part_k == 1:
                    for i in range(NC):
                        mm = pe.matmul(ps_a[:, P * i:P * i + P], w1_sb[:, P * i:P * i + P], xn1T[:],
                                       start=True, stop=True)
                elif part_k == 2:
                    for i in range(NC):
                        mm = pe.matmul(ps_a[:, 0:D], hT[:, i, :], w2_sb[:, i, :], start=(i == 0), stop=(i == NC - 1))
                else:
                    mm = pe.transpose(ps_a[:, 0:P], xn2[:], ident)
                mm.then_inc(pre_mm, 1)

            def scores(b, par, t):
                g, j = divmod(t, UPG)
                u = UPB * b + t
                if t == 0:
                    at_least(pe, k_ready, 32 * (b + 1))
                if j == 0:
                    at_least(pe, q_ready[g], 64 * (b + 1))
                for c in range(NC):
                    if c % 2 == 0:
                        at_least(pe, evacuated, 2 * u + c // 2 - 1)
                    bank = ps_s[:, COLS * c:COLS * c + COLS]
                    for a in range(H // 2):
                        pe.matmul(bank[:, 2 * UQ * a:2 * UQ * (a + 1)], k2[par][:, a, P * c:P * c + P],
                                  qh[:, g, 2 * a:2 * a + 2, UQ * j:UQ * j + UQ],
                                  start=(a == 0), stop=False, skip_group_check=True)
                    if abs(c - g) <= 1:
                        cols = bank.rearrange("p (h q) -> p h q", h=H)
                        for q in range(0, UQ, 2):
                            j0 = P * (c - g) - UQ * j - q + TR0
                            mm = pe.matmul(cols[:, :, q:q + 2], tr[:, j0:j0 + P],
                                           qq[:, g, :, UQ * j + q:UQ * j + q + 2],
                                           start=False, stop=(q == UQ - 2), skip_group_check=True)
                    else:
                        j0 = TRW - P if c > g else 0
                        mm = pe.matmul(bank, tr[:, j0:j0 + P], qq[:, g, :, UQ * j:UQ * j + UQ],
                                       start=False, stop=True, skip_group_check=True)
                    mm.then_inc(scored, 1)

            def values(b, g, G):
                at_least(pe, exped, UPG * (G + 1))
                at_least(pe, att_made, G)
                if g == 0:
                    at_least(pe, v_laid, 8 * (b + 1))
                for c in range(NC):
                    v = v_far if abs(c - g) > 1 else v_pad
                    for hh in range(4):
                        for quad in range(4):
                            h = 4 * quad + hh
                            mm = pe.matmul(ps_o[32 * quad:32 * quad + 32, 0:P], v[:, c, h, :], w[g % 2][:, c, h, :],
                                           start=(c == 0 and hh == 0), stop=False, skip_group_check=True)
                mm.then_inc(v_used, 1)

            def sums(g):
                for c in range(NC):
                    for hh in range(4):
                        for quad in range(4):
                            h = 4 * quad + hh
                            pe.matmul(ps_o[32 * quad:32 * quad + 32, P:2 * P], ones[:, hh, :], w[g % 2][:, c, h, :],
                                      start=False, stop=False, skip_group_check=True)

            def relative(g, G, half):
                at_least(pe, masked, 2 * G + half)
                for op in range(NO // 4):
                    near = [c for c in range(NC) if abs(c - g) <= 1]
                    for c in near:
                        for jj in range(2):
                            oc = NO // 2 * half + 2 * op + jj
                            i0 = P * (c - g) - OCT * oc + TV0 - (OCT - 1)
                            mm = pe.matmul(ps_r[64 * jj:64 * jj + 64, P * op:P * op + P],
                                           tv[:, HD * i0:HD * (i0 + OCT)],
                                           w[g % 2][:, c, :, OCT * oc:OCT * oc + OCT],
                                           start=(c == near[0]), stop=(c == near[-1]))
                mm.then_inc(rel_done, 1)

            def select(G):
                at_least(pe, masked, 2 * G + 2)
                for hh in range(4):
                    for quad in range(4):
                        mm = pe.matmul(ps_o[32 * quad:32 * quad + 32, 0:P], sel[:, hh, :], rown[:, 4 * quad + hh, :],
                                       start=False, stop=(hh == 3), skip_group_check=True)
                mm.then_inc(o_done, 1)

            def after(G, k):
                if k == 0:
                    at_least(pe, att_made, G + 1)
                    at_least(pe, fin_made, G)
                    mm = pe.matmul(ps_b[:, 0:D], attT[:], wo_sb[:], start=True, stop=True)
                elif k == 1:
                    at_least(pe, xn_made[2], G + 1)
                    mm = pe.transpose(ps_b[:, 0:P], xn3[:], ident)
                elif k == 2:
                    at_least(pe, xn3T_made, G + 1)
                    for i in range(NC):
                        mm = pe.matmul(ps_b[:, P * i:P * i + P], w1_sb[:, P * i:P * i + P], xn3T[:],
                                       start=True, stop=True)
                else:
                    at_least(pe, h3_made, G + 1)
                    for i in range(NC):
                        mm = pe.matmul(ps_b[:, 0:D], h3T[:, i, :], w2_sb[:, i, :], start=(i == 0), stop=(i == NC - 1))
                mm.then_inc(post_mm, 1)

            def slot(b, par, t, more):
                g, j = divmod(t, UPG)
                G = NC * b + g
                middle, end = stages_at(t) if more else ([], [])
                if t < UPB:
                    scores(b, par, t)
                for k in middle:
                    stage(b + 1, k)
                if j == 0 and live(G - 2):
                    select(G - 2)
                if j == 1 and live(G - 1):
                    values(b - 1 if g == 0 else b, (g - 1) % NC, G - 1)
                if j == 2 and live(G - 1):
                    sums((g - 1) % NC)
                    relative((g - 1) % NC, G - 1, 0)
                if j == 3 and live(G - 1):
                    relative((g - 1) % NC, G - 1, 1)
                if j == 0 and live(G - 3):
                    after(G - 3, 3)
                if j > 0 and live(G - 2):
                    after(G - 2, j - 1)
                for k in end:
                    stage(b + 1, k)

            pe.wait_ge(c_loaded, 16 * N_LOADS)
            for k in range(NSTAGE):
                stage(0, k)
            pe.wait_ge(tr_step, 11)

            def body(b, par, more):
                for t in range(UPB):
                    slot(b, par, t, more)

            def tail(b):
                for t in range(UPB, UPB + TAIL):
                    slot(b, 1, t, False)

            every_batch(pe, body, tail)

        @block.scalar
        def _(act):
            def stage(b, k):
                if by_act(k) == by_act(k - 1):
                    return
                at_least(act, pre_mm, NSTAGE * b + k + 1)
                j, part_k = divmod(k, 4)
                if k == KEYS:
                    at_least(act, k_split, 4 * b)
                    ins = act.activation(kf[:], ps_a[:], ACT.Identity, bias=bk_sb[:, 0:1])
                elif k == QUERIES:
                    at_least(act, q_split, 4 * b)
                    ins = act.activation(qf[:], ps_a[:], ACT.Identity, bias=bq_sb[:, 0:1])
                elif part_k == 0:
                    ins = act.copy(xn1T[:], ps_a[:, 0:P])
                elif part_k == 1:
                    for i in range(NC):
                        ins = act.activation(hT[:, i, :], ps_a[:, P * i:P * i + P], ACT.Relu, bias=b1_sb[:, i:i + 1])
                else:
                    ins = act.copy(xn2T[:, P * j:P * j + P], ps_a[:, 0:P])
                ins.then_inc(pre_act, 1)

            def evacuate(b, t):
                g, j = divmod(t, UPG)
                u, G = UPB * b + t, NC * b + g
                if j == 0:
                    at_least(act, rel_done, 2 * G - 2)
                for pair in range(2):
                    at_least(act, scored, 4 * u + 2 * pair + 2)
                    dst = w[g % 2][:, 2 * pair:2 * pair + 2, :, UQ * j:UQ * j + UQ].rearrange("p c h q -> p (c h) q")
                    src = ps_s[:, 2 * COLS * pair:2 * COLS * (pair + 1)].rearrange("p (a q) -> p a q", q=UQ)
                    act.copy(dst, src).then_inc(evacuated, 1)

            def exponent(u, t):
                g, j = divmod(t % UPB, UPG)
                at_least(act, shifted, u + 1)
                v = w[g % 2][:, :, :, UQ * j:UQ * j + UQ].rearrange("p c h q -> p (c h) q")
                act.activation(v, v, ACT.Exp, scale=SCALE).then_inc(exped, 1)

            def slot(b, t, more):
                g, j = divmod(t, UPG)
                G = NC * b + g
                middle, end = stages_at(t) if more else ([], [])
                if t < UPB:
                    evacuate(b, t)
                for k in middle:
                    stage(b + 1, k)
                if t <= UPB and not (isinstance(b, int) and UPB * b + t == 0):
                    exponent(UPB * b + t - 1, t - 1)
                if j == 2 and live(G - 2):
                    at_least(act, post_mm, 4 * (G - 2) + 2)
                    act.copy(xn3T[:], ps_b[:, 0:P]).then_inc(xn3T_made, 1)
                if j == 3 and live(G - 2):
                    at_least(act, post_mm, 4 * (G - 2) + 3)
                    for i in range(NC):
                        ins = act.activation(h3T[:, i, :], ps_b[:, P * i:P * i + P], ACT.Relu, bias=b1_sb[:, i:i + 1])
                    ins.then_inc(h3_made, 1)
                for k in end:
                    stage(b + 1, k)

            act.wait_ge(c_loaded, 16 * N_LOADS)
            for k in range(NSTAGE):
                stage(0, k)

            def body(b, par, more):
                for t in range(UPB):
                    slot(b, t, more)

            def tail(b):
                for t in range(UPB, UPB + TAIL):
                    slot(b, t, False)

            every_batch(act, body, tail)

        @block.vector
        def _(dve):
            def statistics(i, n, src):
                dve.bn_stats(st[:, i, :], src).then_inc(stats[i], 1)
                at_least(dve, stats[i], 2 * n + 1)
                stands_alone(dve)
                dve.bn_aggr(mv[:, i, :], st[:, i, :]).then_inc(stats[i], 1)

            def normalise(i, src, dst):
                dve.tensor_scalar(dst, src, mv[:, i, 0:1], rstd[:, i:i + 1],
                                  ALU.subtract, ALU.mult).then_inc(xn_made[i], 1)

            def norm_statistics(b, par, m):
                if m > 0:
                    j = m - 1
                    n = NC * b + j
                    at_least(dve, pre_mm, NSTAGE * b + 4 * j + 3)
                    dve.scalar_tensor_tensor(out=xh[:], in0=ps_a[:, 0:D], scalar=0.5, in1=x_in[:, j, :],
                                             op0=ALU.mult, op1=ALU.add).then_inc(x1_made, 1)
                    at_least(dve, x1_made, 2 * n + 1)
                    dve.tensor_tensor(x1[par][:, j, :], xh[:], b2_half[:], ALU.add).then_inc(x1_made, 1)
                    at_least(dve, x1_made, 2 * n + 2)
                    statistics(1, n, x1[par][:, j, :])
                if m < NC:
                    if m == 0:
                        at_least(dve, x_loaded, 16 * (b + 1))
                    statistics(0, NC * b + m, x_in[:, m, :])
                    at_least(dve, stats[0], 2 * (NC * b + m) + 2)
                if m > 0:
                    at_least(dve, stats[1], 2 * (NC * b + m - 1) + 2)
                dve.tensor_scalar(var[:, 0:2], mv[:, 0:2, 1], EPS, None, ALU.add).then_inc(var_made[0], 1)

            def norm_apply(b, par, m):
                at_least(dve, rstd_made[0], NORMS * b + m + 1)
                if m > 0:
                    normalise(1, x1[par][:, m - 1, :], xn2[:])
                if m < NC:
                    normalise(0, x_in[:, m, :], xn1[:])

            def stage(b, k):
                if k == QUERIES:
                    at_least(dve, pre_act, ACT_STAGES * b + by_act(k))
                    at_least(dve, q_stored, 48 * NP * b)
                    dve.tensor_copy(qp[:, 0, :], qf[:]).then_inc(q_split, 1)
                    at_least(dve, q_split, 4 * b + 1)
                    dve.tensor_tensor(qf[:], qf[:], qp[:, 0, :], ALU.subtract).then_inc(q_split, 1)
                    at_least(dve, q_split, 4 * b + 2)
                    dve.tensor_copy(qp[:, 1, :], qf[:]).then_inc(q_split, 1)
                    at_least(dve, q_split, 4 * b + 3)
                    dve.tensor_tensor(qp[:, 2, :], qf[:], qp[:, 1, :], ALU.subtract).then_inc(q_split, 1)
                elif k == VALUES:
                    at_least(dve, pre_mm, NSTAGE * b + k + 1)
                    at_least(dve, v_laid, 8 * b)
                    dve.tensor_tensor(v_raw[:], ps_a[:].rearrange("p (c d) -> p c d", c=NC),
                                      bv_sb[:].unsqueeze(1).to_broadcast([P, NC, D]), ALU.add).then_inc(v_made, 1)

            def chunk_max(b, t):
                g, j = divmod(t, UPG)
                u = UPB * b + t
                at_least(dve, evacuated, 2 * u + 2)
                v = w[g % 2][:, :, :, UQ * j:UQ * j + UQ]
                at_least(dve, maxed, u)
                dve.tensor_tensor(mtmp[:].rearrange("p c h q -> p (c h) q"),
                                  v[:, 0:2].rearrange("p c h q -> p (c h) q"),
                                  v[:, 2:4].rearrange("p c h q -> p (c h) q"), ALU.max).then_inc(mtmp_made, 1)
                at_least(dve, mtmp_made, u + 1)
                dve.tensor_tensor(mx[:], mtmp[:, 0].rearrange("p h q -> p (h q)"),
                                  mtmp[:, 1].rearrange("p h q -> p (h q)"), ALU.max).then_inc(maxed, 1)

            def shift(u, t):
                g, j = divmod(t % UPB, UPG)
                at_least(dve, max_known, u + 1)
                v = w[g % 2][:, :, :, UQ * j:UQ * j + UQ]
                m = mall[:].rearrange("p (h q) -> p h q", h=H).unsqueeze(1).to_broadcast([P, NC, H, UQ])
                dve.tensor_tensor(v, v, m, ALU.subtract).then_inc(shifted, 1)

            def mask(G, half):
                at_least(dve, rel_done, 2 * G + half + 1)
                if half == 0:
                    at_least(dve, o_done, G)
                r = ps_r[:].rearrange("p (o h q) -> p h o q", h=H, q=OCT)
                for jj in range(2):
                    dst = rown[:, :, 64 * half:64 * half + 64].rearrange("p h (o j q) -> p h o j q", j=2, q=OCT)[:, :, :, jj]
                    m = own[:, jj, :].unsqueeze(1).unsqueeze(1).to_broadcast([P, H, 4, OCT])
                    ins = dve.tensor_tensor(dst, r, m, ALU.mult)
                ins.then_inc(masked, 1)

            def attention(G):
                at_least(dve, o_done, G + 1)
                dve.reciprocal(rden[:], ps_o[:, P:2 * P]).then_inc(rden_made, 1)
                at_least(dve, rden_made, G + 1)
                dve.tensor_tensor(attT[:], ps_o[:, 0:P], rden[:], ALU.mult).then_inc(att_made, 1)

            def residual(G, g, par):
                at_least(dve, post_mm, 4 * G + 1)
                dve.tensor_tensor(xa[:], ps_b[:, 0:D], bo_sb[:], ALU.add).then_inc(x2_made, 1)
                at_least(dve, x2_made, 2 * G + 1)
                dve.tensor_tensor(x2[g % 2][:], xa[:], x1[par][:, g, :], ALU.add).then_inc(x2_made, 1)
                at_least(dve, x2_made, 2 * G + 2)
                statistics(2, G, x2[g % 2][:])
                at_least(dve, stats[2], 2 * G + 2)
                dve.tensor_scalar(var[:, 2:3], mv[:, 2, 1:2], EPS, None, ALU.add).then_inc(var_made[1], 1)

            def finish(G, g, b_last):
                at_least(dve, post_mm, 4 * G + 4)
                dve.scalar_tensor_tensor(out=xf[:], in0=ps_b[:, 0:D], scalar=0.5, in1=x2[g % 2][:],
                                         op0=ALU.mult, op1=ALU.add).then_inc(xf_made, 1)
                at_least(dve, xf_made, G + 1)
                at_least(dve, out_stored[g % 2], 16 * (2 * b_last + g // 2))
                dve.tensor_tensor(out_sb[g % 2][:], xf[:], b2_half[:], ALU.add).then_inc(fin_made, 1)

            def slot(b, par, t, more):
                g, j = divmod(t, UPG)
                G = NC * b + g

                def back(n):
                    q, place = divmod(g - n, NC)
                    return place, (par + q) % 2, b + q

                norm = (t - 1) // 2 if more and t % 2 == 1 and t < 2 * NORMS else None
                if j == 3 and live(G - 1):
                    mask(G - 1, 0)
                if j == 0 and live(G - 2):
                    mask(G - 2, 1)
                if norm is not None:
                    norm_statistics(b + 1, 1 - par, norm)
                if more and t == V_RAW_SLOT:
                    stage(b + 1, VALUES)
                if j == 1 and live(G - 3):
                    place, _, bb = back(3)
                    finish(G - 3, place, bb)
                if j == 2 and live(G - 2):
                    place, pp, _ = back(2)
                    residual(G - 2, place, pp)
                    at_least(dve, rstd_made[1], G - 1)
                    normalise(2, x2[place % 2][:], xn3[:])
                if norm is not None:
                    norm_apply(b + 1, 1 - par, norm)
                if t <= UPB and not (isinstance(b, int) and UPB * b + t == 0):
                    shift(UPB * b + t - 1, t - 1)
                if t < UPB:
                    chunk_max(b, t)
                if more and QUERIES in stages_at(t)[0]:
                    stage(b + 1, QUERIES)
                if j == 0 and live(G - 2):
                    attention(G - 2)

            dve.memset(qe[:], 0.0).then_inc(zeroed, 1)
            dve.memset(qo[:], 0.0).then_inc(zeroed, 1)
            dve.memset(mv[:], 1.0).then_inc(zeroed, 1)
            dve.wait_ge(c_loaded, 16 * N_LOADS)
            dve.tensor_scalar(b2_half[:], b2_sb[:], 0.5, None, ALU.mult).then_inc(half_made, 1)
            dve.wait_ge(zeroed, ZEROED)
            for m in range(NORMS):
                norm_statistics(0, 0, m)
                norm_apply(0, 0, m)
            stage(0, QUERIES)
            stage(0, VALUES)
            for n in range(2):
                rows = slice(HALF * n, HALF * n + HALF)
                a, z = TR0 - REL + n, TR0 + REL + n
                dve.tensor_copy(trf[rows, 0:a], trf[rows, a:a + 1].to_broadcast([HALF, a])).then_inc(tr_step, 1)
                dve.tensor_copy(trf[rows, z + 1:TRW],
                                 trf[rows, z:z + 1].to_broadcast([HALF, TRW - z - 1])).then_inc(tr_step, 1)
            dve.wait_ge(tr_step, 4)
            dve.tensor_copy(trp, trf).then_inc(tr_step, 1)
            dve.wait_ge(tr_step, 5)
            dve.tensor_tensor(trr, trf, trp, ALU.subtract).then_inc(tr_step, 1)
            dve.wait_ge(tr_step, 6)
            dve.tensor_scalar(trf, trp, part[:, 0:1], None, ALU.mult).then_inc(tr_step, 1)
            dve.wait_ge(tr_step, 7)
            dve.tensor_copy(trp, trr).then_inc(tr_step, 1)
            dve.wait_ge(tr_step, 8)
            dve.tensor_tensor(trr, trr, trp, ALU.subtract).then_inc(tr_step, 1)
            dve.wait_ge(tr_step, 9)
            dve.scalar_tensor_tensor(out=trf, in0=trp, scalar=part[:, 1:2], in1=trf,
                                      op0=ALU.mult, op1=ALU.add).then_inc(tr_step, 1)
            dve.wait_ge(tr_step, 10)
            dve.scalar_tensor_tensor(out=tr[:], in0=trr, scalar=part[:, 2:3], in1=trf,
                                      op0=ALU.mult, op1=ALU.add).then_inc(tr_step, 1)

            def body(b, par, more):
                for t in range(UPB):
                    slot(b, par, t, more)

            def tail(b):
                for t in range(UPB, UPB + TAIL):
                    slot(b, 1, t, False)

            every_batch(dve, body, tail)

        @block.gpsimd
        def _(pool):
            def split_keys(b):
                at_least(pool, pre_act, ACT_STAGES * b + by_act(KEYS))
                at_least(pool, k_stored, 16 * NP * b)
                stands_alone(pool)
                pool.tensor_copy(kp[:, 0, :], kf[:]).then_inc(k_split, 1)
                at_least(pool, k_split, 4 * b + 1)
                pool.tensor_tensor(kf[:], kf[:], kp[:, 0, :], ALU.subtract).then_inc(k_split, 1)
                at_least(pool, k_split, 4 * b + 2)
                stands_alone(pool)
                pool.tensor_copy(kp[:, 1, :], kf[:]).then_inc(k_split, 1)
                at_least(pool, k_split, 4 * b + 3)
                pool.tensor_tensor(kp[:, 2, :], kf[:], kp[:, 1, :], ALU.subtract).then_inc(k_split, 1)

            def even_odd(b):
                at_least(pool, q_split, 4 * b + 4)
                at_least(pool, q_stored, 48 * NP * b)
                stands_alone(pool)
                for i, dst in enumerate((qe, qo)):
                    ins = pool.tensor_copy(dst[:].rearrange("p a (s two) -> p a s two", two=2)[:, :, :, i],
                                           qp[:].rearrange("p a (s two) -> p a s two", two=2)[:, :, :, i])
                ins.then_inc(qeo_made, 1)

            def lay_values(b):
                at_least(pool, v_made, b + 1)
                at_least(pool, v_used, NC * b)
                for n in range(2):
                    src = v_raw[:, 2 * n:2 * n + 2, :].rearrange("p c (h d) -> p (c h) d", d=HD)
                    dst = v_sum[:, 2 * n:2 * n + 2, :].rearrange("p c (h d) -> p (c h) d", d=HD)
                    far = relv_far[:, n, :].unsqueeze(1).to_broadcast([P, 2 * H, HD])
                    pool.tensor_tensor(dst, src, far, ALU.add).then_inc(v_sums, 1)
                for n, (src, dst) in enumerate(((v_raw, v_pad), (v_sum, v_far))):
                    if n == 1:
                        at_least(pool, v_sums, 2 * b + 2)
                        stands_alone(pool)
                    for hh in range(4):
                        pool.tensor_copy(
                            dst[:].rearrange("p c (a e) m -> p c a e m", e=4)[:, :, :, hh, HD * hh:HD * hh + HD],
                            src[:].rearrange("p c (a e d) -> p c a e d", e=4, d=HD)[:, :, :, hh, :]).then_inc(v_laid, 1)

            def root(i, n):
                cols = (slice(0, 2), slice(2, 3))[i]
                at_least(pool, var_made[i], n + 1)
                pool.tensor_tensor(rstd[:, cols], var[:, cols], minus_half[:, 0:2 - i], ALU.pow).then_inc(rstd_made[i], 1)

            def slot(b, t, more):
                u = UPB * b + t
                g, j = divmod(t, UPG)
                G = NC * b + g
                if j == 2 and live(G - 2):
                    root(1, G - 2)
                if more and t % 2 == 1 and t < 2 * NORMS:
                    root(0, NORMS * (b + 1) + (t - 1) // 2)
                if t < UPB:
                    at_least(pool, maxed, u + 1)
                    at_least(pool, shifted, u)
                    stands_alone(pool)
                    pool.partition_all_reduce(mall[:], mx[:], P, RMAX).then_inc(max_known, 1)
                if t == V_SLOT:
                    lay_values(b)
                if more and t == K_SLOT:
                    split_keys(b + 1)
                if more and t == Q_SLOT:
                    even_odd(b + 1)

            pool.memset(minus_half[:], -0.5).then_inc(zeroed, 1)
            pool.memset(qh[:], 0.0).then_inc(zeroed, 1)
            pool.memset(v_pad[:], 0.0).then_inc(zeroed, 1)
            pool.memset(v_far[:], 0.0).then_inc(zeroed, 1)
            pool.wait_ge(c_loaded, 16 * N_LOADS)
            pool.wait_ge(zeroed, ZEROED)
            for m in range(NORMS):
                root(0, m)
            split_keys(0)
            even_odd(0)

            def body(b, par, more):
                for t in range(UPB):
                    slot(b, t, more)

            def tail(b):
                for t in range(UPB, UPB + TAIL):
                    slot(b, t, False)

            every_batch(pool, body, tail)


def kernel(**inputs):
    import concourse.bacc as bacc
    from concourse.bass_utils import run_bass_kernel_spmd

    a = {k.removeprefix("L0_"): np.asarray(v) for k, v in inputs.items()}

    def rows(v):
        return np.broadcast_to(v, (P, v.shape[0]))

    arrays = {
        "x": a["attn_x"],
        "wqT": a["attn_Wq"].T, "wkT": a["attn_Wk"].T, "wvT": a["attn_Wv"].T, "woT": a["attn_Wo"].T,
        "bq": a["attn_bq"].reshape(P, 1), "bk": a["attn_bk"].reshape(P, 1),
        "bv": rows(a["attn_bv"]), "bo": rows(a["attn_bo"]),
        "relkT": a["attn_rel_k"].T, "relv": a["attn_rel_v"],
        "w1": a["ffn_W1"], "b1": a["ffn_b1"].reshape(NC, P).T, "w2": a["ffn_W2"], "b2": rows(a["ffn_b2"]),
        "cst": constants(),
    }
    arrays = {k: np.ascontiguousarray(v) for k, v in arrays.items()}
    nc = bacc.Bacc("TRN2", target_bir_lowering=False, num_devices=1)
    args = [nc.dram_tensor(k, v.shape, mybir.dt.from_np(v.dtype), kind="ExternalInput").ap()
            for k, v in arrays.items()]
    out = nc.dram_tensor("out", (B, S, D), F32, kind="ExternalOutput").ap()
    build(nc, *args, out)
    r = run_bass_kernel_spmd(nc, [arrays], core_ids=[0])
    return r.results[0]["out"]
```

```python
from contextlib import ExitStack

import numpy as np

import concourse.bass as bass
from concourse import mybir

F32 = mybir.dt.float32
BF16 = mybir.dt.bfloat16
ALU = mybir.AluOpType
ACT = mybir.ActivationFunctionType
AX = mybir.AxisListType
RMAX = bass.bass_isa.ReduceOp.max

P = 128
B, S, D = 8, 512, 128
H, HD = 16, 8
INTER = 512
REL = 128
NC = S // P
UQ = 32
UPG = P // UQ
UPB = S // UQ
COLS = H * UQ
EPS = 1e-5
SCALE = float(HD) ** -0.5

PAIRS = [(0, 0), (0, 1), (0, 2), (1, 0), (1, 1), (1, 2), (2, 0), (2, 1)]
NP = len(PAIRS)
Q_ROWS = [slice(0, 3), slice(3, 6), slice(6, 8)]
K_ROWS = [slice(0, 7, 3), slice(1, 8, 3), slice(2, 6, 3)]
HALF = NP * HD

TR0, TRW = 512, 1024
TV0 = 2 * P - 1
TVW = 3 * P
OCT = 8
NO = P // OCT

SUM_ROW = 3 * HD


def seat(h):
    return (h // 3, h % 3, 0) if h < 12 else (h - 12, 0, 1)


BY_QUADRANT = sorted(range(H), key=lambda h: (seat(h)[2], seat(h)[1], seat(h)[0]))

UP, DOWN = 1, 2
LAST_T = 3 * NC
KEYS, QUERIES, VALUES = LAST_T + 1, LAST_T + 2, LAST_T + 3
NSTAGE = LAST_T + 4


def by_act(k):
    return sum(1 for s in range(k + 1) if s <= LAST_T and s % 3 != DOWN or s in (KEYS, QUERIES))


ACT_STAGES = by_act(NSTAGE - 1)


def stages_at(t):
    if t % 2 == 0 and 2 <= t <= 2 * NC + 2:
        return [(3 * t // 2 - 3,), (3 * t // 2 - 2,), (3 * t // 2 - 1,)]
    return [(), (VALUES,) if t == VALUES_AT else (), ()]


NORMS = NC + 1
VALUES_AT = 2 * NC + 3
K_SLOT = 2 * NC + 3
Q_SLOT = 2 * NC + 3
QEO_SLOT = Q_SLOT + 2
V_RAW_SLOT = VALUES_AT + 1
V_SLOT = 3
TAIL = 10


def constants():
    p = np.arange(P)
    ident = np.eye(P, dtype=np.float32)
    sel = np.zeros((P, 3, 32), np.float32)
    for place in range(3):
        sel[p, place, HD * place + p % HD] = 1
    spread = np.zeros((P, 2, P), np.float32)
    for region in range(2):
        place = (p % 32) // HD if region == 0 else 0 * p
        spread[p - p % 32 + SUM_ROW + np.where(place < 3, place, 0), region, p] = 1
    own = np.zeros((P, 2, OCT), np.float32)
    own[p, p // 64, 7 - (p % 64) // 8] = 1
    part = np.zeros((P, 3), np.float32)
    part[p, [PAIRS[r % NP][1] for r in p]] = 1
    return np.ascontiguousarray(np.concatenate(
        [ident, spread.reshape(P, -1), sel.reshape(P, -1), own.reshape(P, -1), part], axis=1))


CW = constants().shape[1]
ZEROED = 7


def build(nc, x, wqT, wkT, wvT, woT, bq, bk, bv, bo, relkT, relv, w1, b1, w2, b2, cst, out):
    with ExitStack() as ctx:
        def sb(name, shape, dt=F32):
            return ctx.enter_context(nc.sbuf_tensor(name, shape, dt))

        def ps(name, shape):
            return ctx.enter_context(nc.psum_tensor(name, shape, F32))

        def sem(name):
            return ctx.enter_context(nc.semaphore(name))

        stack_k = nc.dram_tensor("stack_k", (2, H, HD, NP, S), BF16).ap()
        stack_q = nc.dram_tensor("stack_q", (2, H, HD, NP, S), BF16).ap()
        stack_qe = nc.dram_tensor("stack_qe", (2, H, HD, NP, S), BF16).ap()
        stack_qo = nc.dram_tensor("stack_qo", (2, H, HD, NP, S), BF16).ap()
        relv_ext = nc.dram_tensor("relv_ext", (2 * TV0 + 1, HD), F32).ap()

        w1_sb = sb("w1_sb", [P, INTER])
        w2_sb = sb("w2_sb", [P, NC, D])
        wq_sb, wk_sb, wv_sb = (sb(n, [P, D]) for n in ("wq_sb", "wk_sb", "wv_sb"))
        wo_sb = sb("wo_sb", [P, 2, D])
        b1_sb = sb("b1_sb", [P, NC])
        bq_sb, bk_sb = sb("bq_sb", [P, 1]), sb("bk_sb", [P, 1])
        bv_sb, bo_sb, b2_sb = sb("bv_sb", [P, D]), sb("bo_sb", [P, D]), sb("b2_sb", [P, D])
        b2_half = sb("b2_half", [P, D])
        relv_far = sb("relv_far", [P, 2, HD])
        cst_sb = sb("cst_sb", [P, CW])
        ident = cst_sb[:, 0:P]
        spread = cst_sb[:, P:3 * P].rearrange("p (a b) -> p a b", a=2)
        sel = cst_sb[:, 3 * P:3 * P + 96].rearrange("p (a b) -> p a b", a=3)
        own = cst_sb[:, 3 * P + 96:3 * P + 96 + 2 * OCT].rearrange("p (a b) -> p a b", a=2)
        part = cst_sb[:, 3 * P + 96 + 2 * OCT:CW]
        tr = sb("tr", [P, TRW], BF16)
        tv = sb("tv", [P, TVW * HD])

        x_in = sb("x_in", [P, NC, D])
        x1 = [sb(f"x1_{i}", [P, NC, D]) for i in range(2)]
        xn1, xn2, xn3 = sb("xn1", [P, D]), sb("xn2", [P, D]), sb("xn3", [P, D])
        st = sb("st", [P, 3, 6])
        mv = sb("mv", [P, 3, 2])
        var = sb("var", [P, 3])
        rstd = sb("rstd", [P, 3])
        minus_half = sb("minus_half", [P, 2])
        xn1T, xn3T = sb("xn1T", [P, P]), sb("xn3T", [P, P])
        xn2T = sb("xn2T", [P, S])
        hT, h3T = sb("hT", [P, NC, P]), sb("h3T", [P, NC, P])
        xh = sb("xh", [P, D])
        xa = sb("xa", [P, D])
        x2 = [sb(f"x2_{i}", [P, D]) for i in range(2)]
        xf = sb("xf", [P, D])
        out_sb = [sb(f"out_sb{i}", [P, D]) for i in range(2)]

        qf, kf = sb("qf", [P, S]), sb("kf", [P, S])
        qp, kp = sb("qp", [P, 3, S], BF16), sb("kp", [P, 3, S], BF16)
        qe, qo = sb("qe", [P, 3, S], BF16), sb("qo", [P, 3, S], BF16)
        k2 = [sb(f"k2_{i}", [P, H // 2, S], BF16) for i in range(2)]
        qh = sb("qh", [P, 2, H, P], BF16)
        qq = sb("qq", [P, 2, H, P], BF16)
        v_raw, v_sum = sb("v_raw", [P, NC, D]), sb("v_sum", [P, NC, D])
        v_pad = sb("v_pad", [P, NC, H, 32])
        v_far = sb("v_far", [P, NC, H, 32])

        w = [sb(f"weights{i}", [P, NC, H, P]) for i in range(2)]
        mtmp = sb("mtmp", [P, 2, H, UQ])
        mx = [sb(f"mx{i}", [P, COLS]) for i in range(2)]
        mall = [sb(f"mall{i}", [P, COLS]) for i in range(2)]
        rown = sb("rown", [P, H, P])
        trf = rown[:, 0:TRW // P, :].rearrange("p a b -> p (a b)")
        trr = rown[:, TRW // P:2 * TRW // P, :].rearrange("p a b -> p (a b)")
        trp = mtmp[:, 0].rearrange("p h q -> p (h q)").bitcast(BF16)
        o_sb, rden, attT = (sb(n, [P, 2, P]) for n in ("o_sb", "rden", "attT"))

        ps_s = ps("ps_s", [P, NC * COLS])
        ps_r = ps("ps_r", [P, 512])
        ps_o = ps("ps_o", [P, 512])
        ps_a = ps("ps_a", [P, 512])
        ps_b = ps("ps_b", [P, 512])

        c_loaded = sem("c_loaded")
        ext_made = sem("ext_made")
        zeroed = sem("zeroed")
        half_made = sem("half_made")
        tr_step = sem("tr_step")
        x_loaded = sem("x_loaded")
        stats = [sem(f"stats{i}") for i in range(3)]
        var_made = [sem("var_made_pre"), sem("var_made_post")]
        rstd_made = [sem("rstd_made_pre"), sem("rstd_made_post")]
        xn_made = [sem(f"xn_made{i}") for i in range(3)]
        pre_mm = sem("pre_mm")
        pre_act = sem("pre_act")
        x1_made = sem("x1_made")
        q_split, k_split = sem("q_split"), sem("k_split")
        qeo_made = sem("qeo_made")
        v_made = sem("v_made")
        v_sums, v_laid = sem("v_sums"), sem("v_laid")
        k_stored, q_stored = sem("k_stored"), sem("q_stored")
        k_ready = sem("k_ready")
        q_ready = [sem(f"q_ready{i}") for i in range(2)]
        scored = sem("scored")
        evacuated = sem("evacuated")
        mtmp_made, maxed = sem("mtmp_made"), sem("maxed")
        max_known = sem("max_known")
        shifted = sem("shifted")
        exped = sem("exped")
        v_used = sem("v_used")
        rel_done = sem("rel_done")
        masked = sem("masked")
        o_done = sem("o_done")
        o_copied, spread_done = sem("o_copied"), sem("spread_done")
        wo_zeroed, ones_set = sem("wo_zeroed"), sem("ones_set")
        rden_made, att_made = sem("rden_made"), sem("att_made")
        post_mm = sem("post_mm")
        x2_made = sem("x2_made")
        xn3T_made, h3_made = sem("xn3T_made"), sem("h3_made")
        xf_made, fin_made = sem("xf_made"), sem("fin_made")
        wait_held = sem("wait_held")
        out_stored = [sem(f"out_stored{i}") for i in range(2)]

        x_t = x.rearrange("b (t p) d -> b p t d", p=P)
        out_t = out.rearrange("b (t p) d -> b t p d", p=P)
        loads = [
            (w1_sb[:], w1), (w2_sb[:], w2.rearrange("(c p) d -> p c d", p=P)),
            (wq_sb[:], wqT), (wk_sb[:], wkT), (wv_sb[:], wvT),
            (b1_sb[:], b1), (bq_sb[:], bq), (bk_sb[:], bk),
            (bv_sb[:], bv), (bo_sb[:], bo), (b2_sb[:], b2), (cst_sb[:], cst),
        ]
        NEARW = 2 * REL + 1
        for n in range(2):
            j0 = TR0 - REL + n
            for d in range(HD):
                loads.append((trf[HALF * n + NP * d:HALF * n + NP * (d + 1), j0:j0 + NEARW],
                              relkT[d:d + 1, :].to_broadcast([NP, NEARW])))
        far_rows = [relv[0:1, :], relv[2 * REL:2 * REL + 1, :]]
        N_LOADS = len(loads) + 3 + 8

        block = ctx.enter_context(nc.Block())

        def every_batch(e, body, tail):
            body(0, 0, True)
            with e.Fori(0, (B - 2) // 2) as n:
                body(2 * n + 1, 1, True)
                body(2 * n + 2, 0, True)
            body(B - 1, 1, False)
            tail(B - 1)

        def at_least(e, s, n):
            if not isinstance(n, int) or n > 0:
                e.wait_ge(s, n)

        def stands_alone(e):
            e.sem_inc(wait_held, 1)

        def live(G):
            return not isinstance(G, int) or 0 <= G < B * NC

        @block.sync
        def _(sp):
            sp.dma_start(x_in[:], x_t[0]).then_inc(x_loaded, 16)
            mid = TV0 - REL
            sp.dma_start(relv_ext[mid:mid + NEARW, :], relv).then_inc(ext_made, 16)
            sp.dma_start(relv_ext[0:mid, :], bass.AP(relv.tensor, 0, [[0, mid], [1, HD]])).then_inc(ext_made, 16)
            sp.dma_start(relv_ext[mid + NEARW:, :],
                         bass.AP(relv.tensor, 2 * REL * HD, [[0, mid], [1, HD]])).then_inc(ext_made, 16)
            for dst, src in loads:
                sp.dma_start(dst, src).then_inc(c_loaded, 16)
            sp.wait_ge(wo_zeroed, 1)
            for quad in range(4):
                sp.dma_start(wo_sb[32 * quad:32 * quad + SUM_ROW, 0, :],
                             woT[SUM_ROW * quad:SUM_ROW * (quad + 1), :]).then_inc(c_loaded, 16)
                sp.dma_start(wo_sb[32 * quad:32 * quad + HD, 1, :],
                             woT[4 * SUM_ROW + HD * quad:4 * SUM_ROW + HD * (quad + 1), :]).then_inc(c_loaded, 16)
            for n in range(2):
                sp.dma_start(relv_far[:, n, :],
                             bass.AP(relv.tensor, n * 2 * REL * HD, [[0, P], [1, HD]])).then_inc(c_loaded, 16)
            sp.wait_ge(ext_made, 48)
            sp.dma_start(tv[:], bass.AP(relv_ext.tensor, 0, [[HD, P], [1, TVW * HD]])).then_inc(c_loaded, 16)

            def store_stacks(b, par):
                at_least(sp, k_split, 4 * b + 4)
                for i, pairs in enumerate(K_ROWS):
                    sp.dma_start(stack_k[par].rearrange("h d c s -> (h d) c s")[:, pairs],
                                 kp[:, i:i + 1, :].to_broadcast([P, len(range(NP)[pairs]), S])).then_inc(k_stored, 16)
                at_least(sp, qeo_made, b + 1)
                for i, pairs in enumerate(Q_ROWS):
                    for dst, src in ((stack_q, qp), (stack_qe, qe), (stack_qo, qo)):
                        sp.dma_start(dst[par].rearrange("h d c s -> (h d) c s")[:, pairs],
                                     src[:, i:i + 1, :].to_broadcast([P, len(range(NP)[pairs]), S])
                                     ).then_inc(q_stored, 16)
                sp.wait_ge(k_stored, 48 * (b + 1))
                for hp in range(2):
                    sp.dma_start(k2[par][HALF * hp:HALF * hp + HALF],
                                 stack_k[par].rearrange("(a hp) d c s -> hp (d c) a s", hp=2)[hp]).then_inc(k_ready, 16)
                sp.wait_ge(q_stored, 144 * (b + 1))

            def load_queries(b, par, g):
                at_least(sp, scored, 4 * UPG * (NC * b + g - 1))
                q = slice(P * g, P * g + P)
                for hp in range(2):
                    rows = slice(HALF * hp, HALF * hp + HALF)
                    sp.dma_start(qh[rows, g % 2].rearrange("r (a hp) q -> r hp a q", hp=2)[:, hp],
                                 stack_q[par].rearrange("(a hp) d c s -> hp (d c) a s", hp=2)[hp][:, :, q]
                                 ).then_inc(q_ready[g % 2], 16)
                    sp.dma_start(qq[rows, g % 2],
                                 (stack_qe, stack_qo)[hp][par].rearrange("h d c s -> (d c) h s")[:, :, q]
                                 ).then_inc(q_ready[g % 2], 16)

            def store_out(b, back):
                G = NC * b - back
                if not live(G):
                    return
                at_least(sp, fin_made, G + 1)
                stands_alone(sp)
                bb, g = b - (back + NC - 1) // NC, (-back) % NC
                sp.dma_start(out_t[bb, g], out_sb[g % 2][:]).then_inc(out_stored[g % 2], 16)

            sp.wait_ge(zeroed, ZEROED)
            store_stacks(0, 0)
            for g in range(2):
                load_queries(0, 0, g)

            def body(b, par, more):
                if more:
                    at_least(sp, x1_made, 2 * NC * (b + 1))
                    stands_alone(sp)
                    sp.dma_start(x_in[:], x_t[b + 1]).then_inc(x_loaded, 16)
                store_out(b, 3)
                load_queries(b, par, 2)
                store_out(b, 2)
                load_queries(b, par, 3)
                store_out(b, 1)
                if more:
                    store_stacks(b + 1, 1 - par)
                    load_queries(b + 1, 1 - par, 0)
                store_out(b, 0)
                if more:
                    load_queries(b + 1, 1 - par, 1)

            def tail(b):
                for back in (-1, -2, -3):
                    store_out(b, back)
                for i in range(2):
                    sp.wait_ge(out_stored[i], 16 * B * NC // 2)

            every_batch(sp, body, tail)

        @block.tensor
        def _(pe):
            def stage(b, k):
                n = NSTAGE * b + k
                m, part_k = divmod(k, 3)
                if k <= LAST_T and part_k == 0:
                    if m == 0:
                        at_least(pe, v_made, b)
                    else:
                        at_least(pe, xn_made[1], NC * b + m)
                    if m < NC:
                        at_least(pe, xn_made[0], NC * b + m + 1)
                else:
                    at_least(pe, pre_act, ACT_STAGES * b + by_act(k - 1))
                if k == VALUES:
                    for c in range(NC):
                        mm = pe.matmul(ps_a[:, P * c:P * c + P], xn2T[:, P * c:P * c + P], wv_sb[:],
                                       start=True, stop=True)
                elif k > LAST_T:
                    mm = pe.matmul(ps_a[:], (wk_sb if k == KEYS else wq_sb)[:], xn2T[:], start=True, stop=True)
                elif part_k == 0:
                    if m < NC:
                        mm = pe.transpose(ps_a[:, 0:P], xn1[:], ident)
                    if m > 0:
                        mm = pe.transpose(ps_a[:, P:2 * P], xn2[:], ident)
                elif part_k == UP:
                    for i in range(NC):
                        mm = pe.matmul(ps_a[:, P * i:P * i + P], w1_sb[:, P * i:P * i + P], xn1T[:],
                                       start=True, stop=True)
                else:
                    for i in range(NC):
                        mm = pe.matmul(ps_a[:, 0:D], hT[:, i, :], w2_sb[:, i, :], start=(i == 0), stop=(i == NC - 1))
                mm.then_inc(pre_mm, 1)

            def scores(b, par, t):
                g, j = divmod(t, UPG)
                u = UPB * b + t
                if t == 0:
                    at_least(pe, k_ready, 32 * (b + 1))
                if j == 0:
                    at_least(pe, q_ready[g % 2], 64 * (2 * b + g // 2 + 1))
                for c in range(NC):
                    if c % 2 == 0:
                        at_least(pe, evacuated, 2 * u + c // 2 - 1)
                    bank = ps_s[:, COLS * c:COLS * c + COLS]
                    for a in range(H // 2):
                        pe.matmul(bank[:, 2 * UQ * a:2 * UQ * (a + 1)], k2[par][:, a, P * c:P * c + P],
                                  qh[:, g % 2, 2 * a:2 * a + 2, UQ * j:UQ * j + UQ],
                                  start=(a == 0), stop=False, skip_group_check=True)
                    if abs(c - g) <= 1:
                        cols = bank.rearrange("p (h q) -> p h q", h=H)
                        for q in range(0, UQ, 2):
                            j0 = P * (c - g) - UQ * j - q + TR0
                            mm = pe.matmul(cols[:, :, q:q + 2], tr[:, j0:j0 + P],
                                           qq[:, g % 2, :, UQ * j + q:UQ * j + q + 2],
                                           start=False, stop=(q == UQ - 2), skip_group_check=True)
                    else:
                        j0 = TRW - P if c > g else 0
                        mm = pe.matmul(bank, tr[:, j0:j0 + P], qq[:, g % 2, :, UQ * j:UQ * j + UQ],
                                       start=False, stop=True, skip_group_check=True)
                    mm.then_inc(scored, 1)

            def values(b, g, G, half):
                if half == 0:
                    at_least(pe, exped, UPG * (G + 1))
                    at_least(pe, o_copied, G)
                if g == 0:
                    at_least(pe, v_laid, 8 * b + 4 * half + 4)
                for c in range(2 * half, 2 * half + 2):
                    v = v_far if abs(c - g) > 1 else v_pad
                    for n, h in enumerate(BY_QUADRANT):
                        quad, _, region = seat(h)
                        mm = pe.matmul(ps_o[32 * quad:32 * quad + 32, P * region:P * region + P], v[:, c, h, :],
                                       w[g % 2][:, c, h, :], start=(c == 0 and n < 4), stop=False,
                                       skip_group_check=True)
                if half == 1:
                    mm.then_inc(v_used, 1)

            def spread_sums(G):
                at_least(pe, o_copied, G + 1)
                at_least(pe, fin_made, G)
                for region in range(2):
                    mm = pe.matmul(ps_b[:, P * region:P * region + P], spread[:, region, :], o_sb[:, region, :],
                                   start=True, stop=True)
                mm.then_inc(spread_done, 1)

            def relative(g, G, half, ops=range(NO // 4)):
                at_least(pe, masked, 2 * G + half)
                at_least(pe, exped, UPG * G + 2 * (half + 1))
                for op in ops:
                    near = [c for c in range(NC) if abs(c - g) <= 1]
                    for c in near:
                        for jj in range(2):
                            oc = NO // 2 * half + 2 * op + jj
                            i0 = P * (c - g) - OCT * oc + TV0 - (OCT - 1)
                            mm = pe.matmul(ps_r[64 * jj:64 * jj + 64, P * op:P * op + P],
                                           tv[:, HD * i0:HD * (i0 + OCT)],
                                           w[g % 2][:, c, :, OCT * oc:OCT * oc + OCT],
                                           start=(c == near[0]), stop=(c == near[-1]))
                if ops[-1] == NO // 4 - 1:
                    mm.then_inc(rel_done, 1)

            def select(G):
                at_least(pe, masked, 2 * G + 2)
                for h in BY_QUADRANT:
                    quad, place, region = seat(h)
                    mm = pe.matmul(ps_o[32 * quad:32 * quad + 32, P * region:P * region + P], sel[:, place, :],
                                   rown[:, h, :], start=False, stop=(region == 1), skip_group_check=True)
                mm.then_inc(o_done, 1)

            def after(G, k):
                if k == 0:
                    at_least(pe, att_made, G + 1)
                    for region in range(2):
                        mm = pe.matmul(ps_b[:, 0:D], attT[:, region, :], wo_sb[:, region, :],
                                       start=(region == 0), stop=(region == 1))
                elif k == 1:
                    at_least(pe, xn_made[2], G + 1)
                    mm = pe.transpose(ps_b[:, 0:P], xn3[:], ident)
                elif k == 2:
                    at_least(pe, xn3T_made, G + 1)
                    for i in range(NC):
                        mm = pe.matmul(ps_b[:, P * i:P * i + P], w1_sb[:, P * i:P * i + P], xn3T[:],
                                       start=True, stop=True)
                else:
                    at_least(pe, h3_made, G + 1)
                    for i in range(NC):
                        mm = pe.matmul(ps_b[:, 0:D], h3T[:, i, :], w2_sb[:, i, :], start=(i == 0), stop=(i == NC - 1))
                mm.then_inc(post_mm, 1)

            def slot(b, par, t, more):
                g, j = divmod(t, UPG)
                G = NC * b + g
                first, middle, end = stages_at(t) if more else ((), (), ())
                vb, vg = (b - 1 if g == 0 else b), (g - 1) % NC
                for k in first:
                    stage(b + 1, k)
                if t < UPB:
                    scores(b, par, t)
                for k in middle:
                    stage(b + 1, k)
                if j == 0:
                    if live(G - 3):
                        after(G - 3, 3)
                    if live(G - 1):
                        relative(vg, G - 1, 0, range(0, 2))
                    if live(G - 2):
                        select(G - 2)
                elif j == 1:
                    if live(G - 2):
                        spread_sums(G - 2)
                    if live(G - 1):
                        relative(vg, G - 1, 0, range(2, NO // 4))
                        values(vb, vg, G - 1, 0)
                elif j == 2:
                    if live(G - 1):
                        values(vb, vg, G - 1, 1)
                    if live(G - 2):
                        after(G - 2, 0)
                else:
                    if live(G - 2):
                        after(G - 2, 1)
                    if live(G - 1):
                        relative(vg, G - 1, 1)
                    if live(G - 2):
                        after(G - 2, 2)
                for k in end:
                    stage(b + 1, k)

            pe.wait_ge(c_loaded, 16 * N_LOADS)
            for k in range(NSTAGE):
                stage(0, k)
            pe.wait_ge(tr_step, 11)

            def body(b, par, more):
                for t in range(UPB):
                    slot(b, par, t, more)

            def tail(b):
                for t in range(UPB, UPB + TAIL):
                    slot(b, 1, t, False)

            every_batch(pe, body, tail)

        @block.scalar
        def _(act):
            def stage(b, k):
                if by_act(k) == by_act(k - 1):
                    return
                at_least(act, pre_mm, NSTAGE * b + k + 1)
                m, part_k = divmod(k, 3)
                if k == KEYS:
                    at_least(act, k_split, 4 * b)
                    ins = act.activation(kf[:], ps_a[:], ACT.Identity, bias=bk_sb[:, 0:1])
                elif k == QUERIES:
                    at_least(act, q_split, 4 * b)
                    ins = act.activation(qf[:], ps_a[:], ACT.Identity, bias=bq_sb[:, 0:1])
                elif part_k == 0:
                    if m < NC:
                        ins = act.copy(xn1T[:], ps_a[:, 0:P])
                    if m > 0:
                        ins = act.copy(xn2T[:, P * (m - 1):P * m], ps_a[:, P:2 * P])
                else:
                    for i in range(NC):
                        ins = act.activation(hT[:, i, :], ps_a[:, P * i:P * i + P], ACT.Relu, bias=b1_sb[:, i:i + 1])
                ins.then_inc(pre_act, 1)

            def evacuate(b, t):
                g, j = divmod(t, UPG)
                u, G = UPB * b + t, NC * b + g
                if j == 0:
                    at_least(act, rel_done, 2 * G - 2)
                for pair in range(2):
                    at_least(act, scored, 4 * u + 2 * pair + 2)
                    dst = w[g % 2][:, 2 * pair:2 * pair + 2, :, UQ * j:UQ * j + UQ].rearrange("p c h q -> p (c h) q")
                    src = ps_s[:, 2 * COLS * pair:2 * COLS * (pair + 1)].rearrange("p (a q) -> p a q", q=UQ)
                    act.copy(dst, src).then_inc(evacuated, 1)

            def exponent(u, t):
                g, j = divmod(t % UPB, UPG)
                at_least(act, shifted, u + 1)
                v = w[g % 2][:, :, :, UQ * j:UQ * j + UQ].rearrange("p c h q -> p (c h) q")
                act.activation(v, v, ACT.Exp, scale=SCALE).then_inc(exped, 1)

            def even_odd(b):
                at_least(act, q_split, 4 * b + 4)
                at_least(act, q_stored, 144 * b)
                for i, dst in enumerate((qe, qo)):
                    ins = act.copy(dst[:].rearrange("p a (s two) -> p a s two", two=2)[:, :, :, i],
                                   qp[:].rearrange("p a (s two) -> p a s two", two=2)[:, :, :, i])
                ins.then_inc(qeo_made, 1)

            def slot(b, t, more):
                g, j = divmod(t, UPG)
                G = NC * b + g
                first, middle, end = stages_at(t) if more else ((), (), ())
                for k in first:
                    stage(b + 1, k)
                if j == 1 and live(G - 2):
                    at_least(act, o_done, G - 1)
                    act.copy(o_sb[:].rearrange("p r q -> p (r q)"), ps_o[:, 0:2 * P]).then_inc(o_copied, 1)
                if t < UPB:
                    evacuate(b, t)
                for k in middle:
                    stage(b + 1, k)
                if j == 3 and live(G - 2):
                    at_least(act, post_mm, 4 * (G - 2) + 2)
                    act.copy(xn3T[:], ps_b[:, 0:P]).then_inc(xn3T_made, 1)
                if t <= UPB + 1 and not (isinstance(b, int) and UPB * b + t < 2):
                    exponent(UPB * b + t - 2, t - 2)
                if j == 3 and live(G - 2):
                    at_least(act, post_mm, 4 * (G - 2) + 3)
                    for i in range(NC):
                        ins = act.activation(h3T[:, i, :], ps_b[:, P * i:P * i + P], ACT.Relu, bias=b1_sb[:, i:i + 1])
                    ins.then_inc(h3_made, 1)
                for k in end:
                    stage(b + 1, k)
                if more and t == QEO_SLOT:
                    even_odd(b + 1)

            act.wait_ge(c_loaded, 16 * N_LOADS)
            for k in range(NSTAGE):
                stage(0, k)
            even_odd(0)

            def body(b, par, more):
                for t in range(UPB):
                    slot(b, t, more)

            def tail(b):
                for t in range(UPB, UPB + TAIL):
                    slot(b, t, False)

            every_batch(act, body, tail)

        @block.vector
        def _(dve):
            def statistics(i, n, src):
                dve.bn_stats(st[:, i, :], src).then_inc(stats[i], 1)
                at_least(dve, stats[i], 2 * n + 1)
                stands_alone(dve)
                dve.bn_aggr(mv[:, i, :], st[:, i, :]).then_inc(stats[i], 1)

            def normalise(i, src, dst):
                dve.tensor_scalar(dst, src, mv[:, i, 0:1], rstd[:, i:i + 1],
                                  ALU.subtract, ALU.mult).then_inc(xn_made[i], 1)

            def norm_statistics(b, par, m):
                if m > 0:
                    j = m - 1
                    n = NC * b + j
                    at_least(dve, pre_mm, NSTAGE * b + 3 * j + 3)
                    dve.scalar_tensor_tensor(out=xh[:], in0=ps_a[:, 0:D], scalar=0.5, in1=x_in[:, j, :],
                                             op0=ALU.mult, op1=ALU.add).then_inc(x1_made, 1)
                    at_least(dve, x1_made, 2 * n + 1)
                    dve.tensor_tensor(x1[par][:, j, :], xh[:], b2_half[:], ALU.add).then_inc(x1_made, 1)
                    at_least(dve, x1_made, 2 * n + 2)
                    statistics(1, n, x1[par][:, j, :])
                if m < NC:
                    if m == 0:
                        at_least(dve, x_loaded, 16 * (b + 1))
                    statistics(0, NC * b + m, x_in[:, m, :])
                    at_least(dve, stats[0], 2 * (NC * b + m) + 2)
                if m > 0:
                    at_least(dve, stats[1], 2 * (NC * b + m - 1) + 2)
                dve.tensor_scalar(var[:, 0:2], mv[:, 0:2, 1], EPS, None, ALU.add).then_inc(var_made[0], 1)

            def norm_apply(b, par, m):
                at_least(dve, rstd_made[0], NORMS * b + m + 1)
                if m > 0:
                    normalise(1, x1[par][:, m - 1, :], xn2[:])
                if m < NC:
                    normalise(0, x_in[:, m, :], xn1[:])

            def stage(b, k):
                if k == QUERIES:
                    at_least(dve, pre_act, ACT_STAGES * b + by_act(k))
                    at_least(dve, q_stored, 144 * b)
                    dve.tensor_copy(qp[:, 0, :], qf[:]).then_inc(q_split, 1)
                    at_least(dve, q_split, 4 * b + 1)
                    dve.tensor_tensor(qf[:], qf[:], qp[:, 0, :], ALU.subtract).then_inc(q_split, 1)
                    at_least(dve, q_split, 4 * b + 2)
                    dve.tensor_copy(qp[:, 1, :], qf[:]).then_inc(q_split, 1)
                    at_least(dve, q_split, 4 * b + 3)
                    dve.tensor_tensor(qp[:, 2, :], qf[:], qp[:, 1, :], ALU.subtract).then_inc(q_split, 1)
                elif k == VALUES:
                    at_least(dve, pre_mm, NSTAGE * b + k + 1)
                    at_least(dve, v_laid, 8 * b)
                    dve.tensor_tensor(v_raw[:], ps_a[:].rearrange("p (c d) -> p c d", c=NC),
                                      bv_sb[:].unsqueeze(1).to_broadcast([P, NC, D]), ALU.add).then_inc(v_made, 1)

            def chunk_max(b, t):
                g, j = divmod(t, UPG)
                u = UPB * b + t
                at_least(dve, evacuated, 2 * u + 2)
                v = w[g % 2][:, :, :, UQ * j:UQ * j + UQ]
                at_least(dve, maxed, u)
                dve.tensor_tensor(mtmp[:].rearrange("p c h q -> p (c h) q"),
                                  v[:, 0:2].rearrange("p c h q -> p (c h) q"),
                                  v[:, 2:4].rearrange("p c h q -> p (c h) q"), ALU.max).then_inc(mtmp_made, 1)
                at_least(dve, mtmp_made, u + 1)
                dve.tensor_tensor(mx[t % 2][:], mtmp[:, 0].rearrange("p h q -> p (h q)"),
                                  mtmp[:, 1].rearrange("p h q -> p (h q)"), ALU.max).then_inc(maxed, 1)

            def shift(u, t):
                g, j = divmod(t % UPB, UPG)
                at_least(dve, max_known, u + 1)
                v = w[g % 2][:, :, :, UQ * j:UQ * j + UQ]
                m = mall[t % 2][:].rearrange("p (h q) -> p h q", h=H).unsqueeze(1).to_broadcast([P, NC, H, UQ])
                dve.tensor_tensor(v, v, m, ALU.subtract).then_inc(shifted, 1)

            def mask(G, half):
                at_least(dve, rel_done, 2 * G + half + 1)
                if half == 0:
                    at_least(dve, o_done, G)
                r = ps_r[:].rearrange("p (o h q) -> p h o q", h=H, q=OCT)
                for jj in range(2):
                    dst = rown[:, :, 64 * half:64 * half + 64].rearrange("p h (o j q) -> p h o j q", j=2, q=OCT)[:, :, :, jj]
                    m = own[:, jj, :].unsqueeze(1).unsqueeze(1).to_broadcast([P, H, 4, OCT])
                    ins = dve.tensor_tensor(dst, r, m, ALU.mult)
                ins.then_inc(masked, 1)

            def attention(G):
                at_least(dve, spread_done, G + 1)
                dve.reciprocal(rden[:].rearrange("p r q -> p (r q)"), ps_b[:, 0:2 * P]).then_inc(rden_made, 1)
                at_least(dve, rden_made, G + 1)
                dve.tensor_tensor(attT[:], o_sb[:], rden[:], ALU.mult).then_inc(att_made, 1)

            def residual(G, g, par):
                at_least(dve, post_mm, 4 * G + 1)
                dve.tensor_tensor(xa[:], ps_b[:, 0:D], bo_sb[:], ALU.add).then_inc(x2_made, 1)
                at_least(dve, x2_made, 2 * G + 1)
                dve.tensor_tensor(x2[g % 2][:], xa[:], x1[par][:, g, :], ALU.add).then_inc(x2_made, 1)
                at_least(dve, x2_made, 2 * G + 2)
                statistics(2, G, x2[g % 2][:])
                at_least(dve, stats[2], 2 * G + 2)
                dve.tensor_scalar(var[:, 2:3], mv[:, 2, 1:2], EPS, None, ALU.add).then_inc(var_made[1], 1)

            def finish(G, g, b_last):
                at_least(dve, post_mm, 4 * G + 4)
                dve.scalar_tensor_tensor(out=xf[:], in0=ps_b[:, 0:D], scalar=0.5, in1=x2[g % 2][:],
                                         op0=ALU.mult, op1=ALU.add).then_inc(xf_made, 1)
                at_least(dve, xf_made, G + 1)
                at_least(dve, out_stored[g % 2], 16 * (2 * b_last + g // 2))
                dve.tensor_tensor(out_sb[g % 2][:], xf[:], b2_half[:], ALU.add).then_inc(fin_made, 1)

            def slot(b, par, t, more):
                g, j = divmod(t, UPG)
                G = NC * b + g

                def back(n):
                    q, place = divmod(g - n, NC)
                    return place, (par + q) % 2, b + q

                norm = (t - 1) // 2 if more and t % 2 == 1 and t < 2 * NORMS else None
                if j == 0 and live(G - 2):
                    mask(G - 2, 1)
                if j == 1 and live(G - 3):
                    place, _, bb = back(3)
                    finish(G - 3, place, bb)
                if j == 2 and live(G - 1):
                    mask(G - 1, 0)
                if j == 2 and live(G - 2):
                    attention(G - 2)
                if norm is not None:
                    norm_statistics(b + 1, 1 - par, norm)
                if j == 3 and live(G - 2):
                    place, pp, _ = back(2)
                    residual(G - 2, place, pp)
                if norm is not None:
                    norm_apply(b + 1, 1 - par, norm)
                if j == 3 and live(G - 2):
                    at_least(dve, rstd_made[1], G - 1)
                    normalise(2, x2[back(2)[0] % 2][:], xn3[:])
                if more and t == Q_SLOT:
                    stage(b + 1, QUERIES)
                if more and t == V_RAW_SLOT:
                    stage(b + 1, VALUES)
                if t < UPB:
                    chunk_max(b, t)
                if t <= UPB and not (isinstance(b, int) and UPB * b + t == 0):
                    shift(UPB * b + t - 1, t - 1)

            dve.memset(wo_sb[:], 0.0).then_inc(wo_zeroed, 1)
            dve.memset(qe[:], 0.0).then_inc(zeroed, 1)
            dve.memset(qo[:], 0.0).then_inc(zeroed, 1)
            dve.memset(mv[:], 1.0).then_inc(zeroed, 1)
            dve.wait_ge(c_loaded, 16 * N_LOADS)
            dve.tensor_scalar(b2_half[:], b2_sb[:], 0.5, None, ALU.mult).then_inc(half_made, 1)
            dve.wait_ge(zeroed, ZEROED)
            for m in range(NORMS):
                norm_statistics(0, 0, m)
                norm_apply(0, 0, m)
            stage(0, QUERIES)
            stage(0, VALUES)
            for n in range(2):
                rows = slice(HALF * n, HALF * n + HALF)
                a, z = TR0 - REL + n, TR0 + REL + n
                dve.tensor_copy(trf[rows, 0:a], trf[rows, a:a + 1].to_broadcast([HALF, a])).then_inc(tr_step, 1)
                dve.tensor_copy(trf[rows, z + 1:TRW],
                                 trf[rows, z:z + 1].to_broadcast([HALF, TRW - z - 1])).then_inc(tr_step, 1)
            dve.wait_ge(tr_step, 4)
            dve.tensor_copy(trp, trf).then_inc(tr_step, 1)
            dve.wait_ge(tr_step, 5)
            dve.tensor_tensor(trr, trf, trp, ALU.subtract).then_inc(tr_step, 1)
            dve.wait_ge(tr_step, 6)
            dve.tensor_scalar(trf, trp, part[:, 0:1], None, ALU.mult).then_inc(tr_step, 1)
            dve.wait_ge(tr_step, 7)
            dve.tensor_copy(trp, trr).then_inc(tr_step, 1)
            dve.wait_ge(tr_step, 8)
            dve.tensor_tensor(trr, trr, trp, ALU.subtract).then_inc(tr_step, 1)
            dve.wait_ge(tr_step, 9)
            dve.scalar_tensor_tensor(out=trf, in0=trp, scalar=part[:, 1:2], in1=trf,
                                      op0=ALU.mult, op1=ALU.add).then_inc(tr_step, 1)
            dve.wait_ge(tr_step, 10)
            dve.scalar_tensor_tensor(out=tr[:], in0=trr, scalar=part[:, 2:3], in1=trf,
                                      op0=ALU.mult, op1=ALU.add).then_inc(tr_step, 1)

            def body(b, par, more):
                for t in range(UPB):
                    slot(b, par, t, more)

            def tail(b):
                for t in range(UPB, UPB + TAIL):
                    slot(b, 1, t, False)

            every_batch(dve, body, tail)

        @block.gpsimd
        def _(pool):
            def split_keys(b, part):
                if part == 0:
                    at_least(pool, pre_act, ACT_STAGES * b + by_act(KEYS))
                    at_least(pool, k_stored, 48 * b)
                    stands_alone(pool)
                    pool.tensor_copy(kp[:, 0, :], kf[:]).then_inc(k_split, 1)
                    at_least(pool, k_split, 4 * b + 1)
                    pool.tensor_tensor(kf[:], kf[:], kp[:, 0, :], ALU.subtract).then_inc(k_split, 1)
                else:
                    at_least(pool, k_split, 4 * b + 2)
                    stands_alone(pool)
                    pool.tensor_copy(kp[:, 1, :], kf[:]).then_inc(k_split, 1)
                    at_least(pool, k_split, 4 * b + 3)
                    pool.tensor_tensor(kp[:, 2, :], kf[:], kp[:, 1, :], ALU.subtract).then_inc(k_split, 1)

            def sum_values(b, n):
                at_least(pool, v_made, b + 1)
                src = v_raw[:, 2 * n:2 * n + 2, :].rearrange("p c (h d) -> p (c h) d", d=HD)
                dst = v_sum[:, 2 * n:2 * n + 2, :].rearrange("p c (h d) -> p (c h) d", d=HD)
                far = relv_far[:, n, :].unsqueeze(1).to_broadcast([P, 2 * H, HD])
                pool.tensor_tensor(dst, src, far, ALU.add).then_inc(v_sums, 1)

            def lay_values(b, n):
                src, dst = ((v_raw, v_pad), (v_sum, v_far))[n]
                at_least(pool, v_used, NC * b)
                at_least(pool, v_sums, 2 * b + 2)
                stands_alone(pool)
                for place in range(4):
                    lo, hi, step = (place, 12, 3) if place < 3 else (12, H, 1)
                    c0 = HD * (place % 3)
                    pool.tensor_copy(
                        dst[:, :, lo:hi:step, c0:c0 + HD],
                        src[:].rearrange("p c (h d) -> p c h d", d=HD)[:, :, lo:hi:step, :]).then_inc(v_laid, 1)

            def root(i, n):
                cols = (slice(0, 2), slice(2, 3))[i]
                at_least(pool, var_made[i], n + 1)
                pool.tensor_tensor(rstd[:, cols], var[:, cols], minus_half[:, 0:2 - i], ALU.pow).then_inc(rstd_made[i], 1)

            def slot(b, t, more):
                u = UPB * b + t
                g, j = divmod(t, UPG)
                G = NC * b + g
                if more and t % 2 == 1 and t < 2 * NORMS:
                    root(0, NORMS * (b + 1) + (t - 1) // 2)
                if j == 3 and live(G - 2):
                    root(1, G - 2)
                if t < UPB:
                    at_least(pool, maxed, u + 1)
                    at_least(pool, shifted, u - 1)
                    stands_alone(pool)
                    pool.partition_all_reduce(mall[t % 2][:], mx[t % 2][:], P, RMAX).then_inc(max_known, 1)
                for n in range(2):
                    if t == V_SLOT + n - 2:
                        sum_values(b, n)
                    if t == V_SLOT + n:
                        lay_values(b, n)
                    if more and t == K_SLOT + n:
                        split_keys(b + 1, n)

            pool.memset(minus_half[:], -0.5).then_inc(zeroed, 1)
            pool.memset(qh[:], 0.0).then_inc(zeroed, 1)
            pool.memset(v_pad[:], 0.0).then_inc(ones_set, 1)
            pool.memset(v_far[:], 0.0).then_inc(ones_set, 1)
            pool.wait_ge(ones_set, 2)
            for dst in (v_pad, v_far):
                for place in range(4):
                    lo, hi, step = (place, 12, 3) if place < 3 else (12, H, 1)
                    c1 = SUM_ROW + place % 3
                    ins = pool.memset(dst[:, :, lo:hi:step, c1:c1 + 1], 1.0)
                ins.then_inc(zeroed, 1)
            pool.wait_ge(c_loaded, 16 * N_LOADS)
            pool.wait_ge(zeroed, ZEROED)
            for m in range(NORMS):
                root(0, m)
            for n in range(2):
                split_keys(0, n)

            def body(b, par, more):
                for t in range(UPB):
                    slot(b, t, more)

            def tail(b):
                for t in range(UPB, UPB + TAIL):
                    slot(b, t, False)

            every_batch(pool, body, tail)


def kernel(**inputs):
    import concourse.bacc as bacc
    from concourse.bass_utils import run_bass_kernel_spmd

    a = {k.removeprefix("L0_"): np.asarray(v) for k, v in inputs.items()}

    def rows(v):
        return np.broadcast_to(v, (P, v.shape[0]))

    arrays = {
        "x": a["attn_x"],
        "wqT": a["attn_Wq"].T, "wkT": a["attn_Wk"].T, "wvT": a["attn_Wv"].T, "woT": a["attn_Wo"].T,
        "bq": a["attn_bq"].reshape(P, 1), "bk": a["attn_bk"].reshape(P, 1),
        "bv": rows(a["attn_bv"]), "bo": rows(a["attn_bo"]),
        "relkT": a["attn_rel_k"].T, "relv": a["attn_rel_v"],
        "w1": a["ffn_W1"], "b1": a["ffn_b1"].reshape(NC, P).T, "w2": a["ffn_W2"], "b2": rows(a["ffn_b2"]),
        "cst": constants(),
    }
    arrays = {k: np.ascontiguousarray(v) for k, v in arrays.items()}
    nc = bacc.Bacc("TRN2", target_bir_lowering=False, num_devices=1)
    args = [nc.dram_tensor(k, v.shape, mybir.dt.from_np(v.dtype), kind="ExternalInput").ap()
            for k, v in arrays.items()]
    out = nc.dram_tensor("out", (B, S, D), F32, kind="ExternalOutput").ap()
    build(nc, *args, out)
    r = run_bass_kernel_spmd(nc, [arrays], core_ids=[0])
    return r.results[0]["out"]
```

```python
from contextlib import ExitStack

import numpy as np

import concourse.bass as bass
from concourse import mybir

F32 = mybir.dt.float32
BF16 = mybir.dt.bfloat16
ALU = mybir.AluOpType
ACT = mybir.ActivationFunctionType
AX = mybir.AxisListType
RMAX = bass.bass_isa.ReduceOp.max

P = 128
B, S, D = 8, 512, 128
H, HD = 16, 8
INTER = 512
REL = 128
NC = S // P
UQ = 32
UPG = P // UQ
UPB = S // UQ
COLS = H * UQ
EPS = 1e-5
SCALE = float(HD) ** -0.5

PAIRS = [(0, 0), (0, 1), (0, 2), (1, 0), (1, 1), (1, 2), (2, 0), (2, 1)]
NP = len(PAIRS)
Q_ROWS = [slice(0, 3), slice(3, 6), slice(6, 8)]
K_ROWS = [slice(0, 7, 3), slice(1, 8, 3), slice(2, 6, 3)]
HALF = NP * HD

TR0, TRW = 512, 1024
TV0 = 2 * P - 1
TVW = 3 * P
OCT = 8
NO = P // OCT

SUM_ROW = 3 * HD


def seat(h):
    return (h // 3, h % 3, 0) if h < 12 else (h - 12, 0, 1)


BY_QUADRANT = sorted(range(H), key=lambda h: (seat(h)[2], seat(h)[1], seat(h)[0]))

UP, DOWN = 1, 2
LAST_T = 3 * NC
KEYS, QUERIES, VALUES = LAST_T + 1, LAST_T + 2, LAST_T + 3
NSTAGE = LAST_T + 4


def by_act(k):
    return sum(1 for s in range(k + 1) if s <= LAST_T and s % 3 != DOWN or s in (KEYS, QUERIES))


ACT_STAGES = by_act(NSTAGE - 1)


def stages_at(t):
    if t % 2 == 0 and 2 <= t <= 2 * NC + 2:
        return [(3 * t // 2 - 3,), (3 * t // 2 - 2,), (3 * t // 2 - 1,)]
    return [(), (VALUES,) if t == VALUES_AT else (), ()]


NORMS = NC + 1
VALUES_AT = 2 * NC + 3
K_SLOT = 2 * NC + 3
Q_SLOT = 2 * NC + 3
QEO_SLOT = Q_SLOT + 1
V_RAW_SLOT = VALUES_AT + 1
V_SLOT = 3
POOL_CHUNK = 3
TAIL = 10


def constants():
    p = np.arange(P)
    ident = np.eye(P, dtype=np.float32)
    sel = np.zeros((P, 3, 32), np.float32)
    for place in range(3):
        sel[p, place, HD * place + p % HD] = 1
    spread = np.zeros((P, 2, P), np.float32)
    gather = np.zeros((P, 2, P), np.float32)
    for h in range(H):
        quad, place, region = seat(h)
        for d in range(HD):
            spread[32 * quad + SUM_ROW + place, region, HD * h + d] = 1
            gather[32 * quad + HD * place + d, region, HD * h + d] = 1
    own = np.zeros((P, 2, OCT), np.float32)
    own[p, p // 64, 7 - (p % 64) // 8] = 1
    part = np.zeros((P, 3), np.float32)
    part[p, [PAIRS[r % NP][1] for r in p]] = 1
    return np.ascontiguousarray(np.concatenate(
        [ident, spread.reshape(P, -1), gather.reshape(P, -1), sel.reshape(P, -1), own.reshape(P, -1), part], axis=1))


CW = constants().shape[1]
ZEROED = 7


def build(nc, x, wqT, wkT, wvT, woT, bq, bk, bv, bo, relkT, relv, w1, b1, w2, b2, cst, out):
    with ExitStack() as ctx:
        def sb(name, shape, dt=F32):
            return ctx.enter_context(nc.sbuf_tensor(name, shape, dt))

        def ps(name, shape):
            return ctx.enter_context(nc.psum_tensor(name, shape, F32))

        def sem(name):
            return ctx.enter_context(nc.semaphore(name))

        stack_k = nc.dram_tensor("stack_k", (2, H, HD, NP, S), BF16).ap()
        stack_q = nc.dram_tensor("stack_q", (2, H, HD, NP, S), BF16).ap()
        stack_qe = nc.dram_tensor("stack_qe", (2, H, HD, NP, S), BF16).ap()
        stack_qo = nc.dram_tensor("stack_qo", (2, H, HD, NP, S), BF16).ap()
        relv_ext = nc.dram_tensor("relv_ext", (2 * TV0 + 1, HD), F32).ap()

        w1_sb = sb("w1_sb", [P, INTER])
        w2_sb = sb("w2_sb", [P, NC, D])
        wq_sb, wk_sb, wv_sb, wo_sb = (sb(n, [P, D]) for n in ("wq_sb", "wk_sb", "wv_sb", "wo_sb"))
        b1_sb = sb("b1_sb", [P, NC])
        bq_sb, bk_sb = sb("bq_sb", [P, 1]), sb("bk_sb", [P, 1])
        bv_sb, bo_sb, b2_sb = sb("bv_sb", [P, D]), sb("bo_sb", [P, D]), sb("b2_sb", [P, D])
        b2_half = sb("b2_half", [P, D])
        relv_far = sb("relv_far", [P, 2, HD])
        cst_sb = sb("cst_sb", [P, CW])
        ident = cst_sb[:, 0:P]
        spread = cst_sb[:, P:3 * P].rearrange("p (a b) -> p a b", a=2)
        gather = cst_sb[:, 3 * P:5 * P].rearrange("p (a b) -> p a b", a=2)
        sel = cst_sb[:, 5 * P:5 * P + 96].rearrange("p (a b) -> p a b", a=3)
        own = cst_sb[:, 5 * P + 96:5 * P + 96 + 2 * OCT].rearrange("p (a b) -> p a b", a=2)
        part = cst_sb[:, 5 * P + 96 + 2 * OCT:CW]
        tr = sb("tr", [P, TRW], BF16)
        tv = sb("tv", [P, TVW * HD])

        x_in = sb("x_in", [P, NC, D])
        x1 = [sb(f"x1_{i}", [P, NC, D]) for i in range(2)]
        xn1, xn2, xn3 = sb("xn1", [P, D]), sb("xn2", [P, D]), sb("xn3", [P, D])
        st = sb("st", [P, 3, 6])
        mv = sb("mv", [P, 3, 2])
        var = sb("var", [P, 3])
        rstd = sb("rstd", [P, 3])
        minus_half = sb("minus_half", [P, NC])
        st4, mv4 = sb("st4", [P, NC, 6]), sb("mv4", [P, NC, 2])
        warm = sb("warm", [P, 1])
        var4, rstd4 = sb("var4", [P, NC]), sb("rstd4", [P, NC])
        xn1T, xn3T = sb("xn1T", [P, P]), sb("xn3T", [P, P])
        xn2T = sb("xn2T", [P, S])
        hT, h3T = sb("hT", [P, NC, P]), sb("h3T", [P, NC, P])
        xb = sb("xb", [P, NC, D])
        x2 = [sb(f"x2_{i}", [P, D]) for i in range(2)]
        out_sb = [sb(f"out_sb{i}", [P, D]) for i in range(2)]

        qf, kf = sb("qf", [P, S]), sb("kf", [P, S])
        qp, kp = sb("qp", [P, 3, S], BF16), sb("kp", [P, 3, S], BF16)
        qe, qo = sb("qe", [P, 3, S], BF16), sb("qo", [P, 3, S], BF16)
        k2 = [sb(f"k2_{i}", [P, H // 2, S], BF16) for i in range(2)]
        qh = sb("qh", [P, 2, H, P], BF16)
        qq = sb("qq", [P, 2, H, P], BF16)
        v_raw, v_sum = sb("v_raw", [P, NC, D]), sb("v_sum", [P, NC, D])
        v_pad = sb("v_pad", [P, NC, H, 32])
        v_far = sb("v_far", [P, NC, H, 32])

        w = [sb(f"weights{i}", [P, NC, H, P]) for i in range(2)]
        mtmp = sb("mtmp", [P, 2, H, UQ])
        mx = [sb(f"mx{i}", [P, COLS]) for i in range(2)]
        mall = [sb(f"mall{i}", [P, COLS]) for i in range(2)]
        rown = sb("rown", [P, H, P])
        trf = w[1][:, 0, 0:H // 2, :].rearrange("p a b -> p (a b)")
        trr = w[1][:, 0, H // 2:H, :].rearrange("p a b -> p (a b)")
        trp = w[1][:, 1, 0:H // 4, :].rearrange("p a b -> p (a b)").bitcast(BF16)
        xn4 = [w[0][:, 0, NC * i:NC * i + NC, :] for i in range(2)]
        xn4T = w[0][:, 0, 2 * NC:3 * NC, :].rearrange("p a b -> p (a b)")
        h4T = w[0][:, 1].rearrange("p (i m) t -> p i (m t)", m=NC)
        o_sb = sb("o_sb", [P, 2, P])
        rden, attT = sb("rden", [P, P]), sb("attT", [P, P])

        ps_s = ps("ps_s", [P, NC * COLS])
        ps_r = ps("ps_r", [P, 512])
        ps_o = ps("ps_o", [P, 512])
        ps_a = ps("ps_a", [P, 512])
        ps_b = ps("ps_b", [P, 512])

        f_loaded = sem("f_loaded")
        c_loaded = sem("c_loaded")
        ext_made = sem("ext_made")
        first_stats, first_var = sem("first_stats"), sem("first_var")
        first_root, first_xn = sem("first_root"), sem("first_xn")
        first_mm, first_act = sem("first_mm"), sem("first_act")
        zeroed = sem("zeroed")
        half_made = sem("half_made")
        tr_step = sem("tr_step")
        x_loaded = sem("x_loaded")
        stats = [sem(f"stats{i}") for i in range(3)]
        var_made = [sem("var_made_pre"), sem("var_made_post")]
        rstd_made = [sem("rstd_made_pre"), sem("rstd_made_post")]
        xn_made = [sem(f"xn_made{i}") for i in range(3)]
        pre_mm = sem("pre_mm")
        pre_act = sem("pre_act")
        xb_made = sem("xb_made")
        x1_made = sem("x1_made")
        x1_biased = sem("x1_biased")
        x2_biased = sem("x2_biased")
        q_split, k_split = sem("q_split"), sem("k_split")
        qeo_made = sem("qeo_made")
        v_made = sem("v_made")
        v_sums = sem("v_sums")
        v_laid = [sem("v_laid"), sem("v_far_laid")]
        k_stored = sem("k_stored")
        q_stored = [sem(f"q_stored{i}") for i in range(2)]
        k_ready = sem("k_ready")
        q_ready = [sem(f"q_ready{i}") for i in range(2)]
        scored = sem("scored")
        evacuated = sem("evacuated")
        mtmp_made, maxed = sem("mtmp_made"), sem("maxed")
        max_known = sem("max_known")
        shifted = sem("shifted")
        pool_shifted = sem("pool_shifted")
        exped = sem("exped")
        v_used = sem("v_used")
        rel_done = sem("rel_done")
        masked = [sem("masked_even"), sem("masked_odd")]
        o_done = sem("o_done")
        o_copied, compacted = sem("o_copied"), sem("compacted")
        ones_set = sem("ones_set")
        rden_made, att_made = sem("rden_made"), sem("att_made")
        post_mm = sem("post_mm")
        x2_made = sem("x2_made")
        xn3T_made, h3_made = sem("xn3T_made"), sem("h3_made")
        fin_made = sem("fin_made")
        wait_held = sem("wait_held")
        out_stored = [sem(f"out_stored{i}") for i in range(2)]

        x_t = x.rearrange("b (t p) d -> b p t d", p=P)
        out_t = out.rearrange("b (t p) d -> b t p d", p=P)
        ffn_loads = [(cst_sb[:], cst), (w1_sb[:], w1), (b1_sb[:], b1),
                     (w2_sb[:], w2.rearrange("(c p) d -> p c d", p=P)), (b2_sb[:], b2), (bo_sb[:], bo)]
        loads = [
            (wq_sb[:], wqT), (wk_sb[:], wkT), (wv_sb[:], wvT), (wo_sb[:], woT),
            (bq_sb[:], bq), (bk_sb[:], bk), (bv_sb[:], bv),
        ]
        NEARW = 2 * REL + 1
        for n in range(2):
            j0 = TR0 - REL + n
            for d in range(HD):
                loads.append((trf[HALF * n + NP * d:HALF * n + NP * (d + 1), j0:j0 + NEARW],
                              relkT[d:d + 1, :].to_broadcast([NP, NEARW])))
        far_rows = [relv[0:1, :], relv[2 * REL:2 * REL + 1, :]]
        N_LOADS = len(loads) + 3

        block = ctx.enter_context(nc.Block())

        def every_batch(e, body, tail):
            body(0, 0, True)
            with e.Fori(0, (B - 2) // 2) as n:
                body(2 * n + 1, 1, True)
                body(2 * n + 2, 0, True)
            body(B - 1, 1, False)
            tail(B - 1)

        def at_least(e, s, n):
            if not isinstance(n, int) or n > 0:
                e.wait_ge(s, n)

        def stands_alone(e):
            e.sem_inc(wait_held, 1)

        def live(G):
            return not isinstance(G, int) or 0 <= G < B * NC

        def lay_values(e, b, n):
            src, dst, copy = ((v_raw, v_pad, nc.gpsimd.tensor_copy), (v_sum, v_far, nc.scalar.copy))[n]
            at_least(e, v_used, NC * b)
            at_least(e, v_sums, 2 * b + 2)
            stands_alone(e)
            for place in range(4):
                lo, hi, step = (place, 12, 3) if place < 3 else (12, H, 1)
                c0 = HD * (place % 3)
                copy(dst[:, :, lo:hi:step, c0:c0 + HD],
                     src[:].rearrange("p c (h d) -> p c h d", d=HD)[:, :, lo:hi:step, :]).then_inc(v_laid[n], 1)

        def mask(e, G, half, jj):
            at_least(e, rel_done, 2 * G + half + 1)
            if half == 0:
                at_least(e, o_done, G)
            own_cols = rown[:, :, 64 * half:64 * half + 64].rearrange("p h (o j q) -> p h o j q", j=2, q=OCT)
            e.tensor_tensor(own_cols[:, :, :, jj], ps_r[:].rearrange("p (o h q) -> p h o q", h=H, q=OCT),
                            own[:, jj, :].unsqueeze(1).unsqueeze(1).to_broadcast([P, H, 4, OCT]),
                            ALU.mult).then_inc(masked[jj], 1)

        def shift(e, share, u, t):
            g, j = divmod(t % UPB, UPG)
            at_least(e, max_known, u + 1)
            first, last, done = ((0, POOL_CHUNK, shifted), (POOL_CHUNK, NC, pool_shifted))[share]
            v = w[g % 2][:, first:last, :, UQ * j:UQ * j + UQ]
            m = mall[t % 2][:].rearrange("p (h q) -> p h q", h=H).unsqueeze(1).to_broadcast([P, last - first, H, UQ])
            e.tensor_tensor(v, v, m, ALU.subtract).then_inc(done, 1)

        def split_keys(e, b):
            at_least(e, pre_act, ACT_STAGES * b + by_act(KEYS))
            e.tensor_tensor(kf[:], kf[:], kp[:, 0, :], ALU.subtract).then_inc(k_split, 1)
            at_least(e, k_split, 3 * b + 1)
            stands_alone(e)
            e.tensor_copy(kp[:, 1, :], kf[:]).then_inc(k_split, 1)
            at_least(e, k_split, 3 * b + 2)
            e.tensor_tensor(kp[:, 2, :], kf[:], kp[:, 1, :], ALU.subtract).then_inc(k_split, 1)

        @block.sync
        def _(sp):
            sp.dma_start(x_in[:], x_t[0]).then_inc(x_loaded, 16)
            for dst, src in ffn_loads:
                sp.dma_start(dst, src).then_inc(f_loaded, 16)
            mid = TV0 - REL
            sp.dma_start(relv_ext[mid:mid + NEARW, :], relv).then_inc(ext_made, 16)
            sp.dma_start(relv_ext[0:mid, :], bass.AP(relv.tensor, 0, [[0, mid], [1, HD]])).then_inc(ext_made, 16)
            sp.dma_start(relv_ext[mid + NEARW:, :],
                         bass.AP(relv.tensor, 2 * REL * HD, [[0, mid], [1, HD]])).then_inc(ext_made, 16)
            for dst, src in loads:
                sp.dma_start(dst, src).then_inc(c_loaded, 16)
            for n in range(2):
                sp.dma_start(relv_far[:, n, :],
                             bass.AP(relv.tensor, n * 2 * REL * HD, [[0, P], [1, HD]])).then_inc(c_loaded, 16)
            sp.wait_ge(ext_made, 48)
            sp.dma_start(tv[:], bass.AP(relv_ext.tensor, 0, [[HD, P], [1, TVW * HD]])).then_inc(c_loaded, 16)

            def store_stacks(b, par):
                at_least(sp, k_split, 3 * b + 3)
                for i, pairs in enumerate(K_ROWS):
                    sp.dma_start(stack_k[par].rearrange("h d c s -> (h d) c s")[:, pairs],
                                 kp[:, i:i + 1, :].to_broadcast([P, len(range(NP)[pairs]), S])).then_inc(k_stored, 16)
                at_least(sp, qeo_made, b + 1)
                store_queries(par, 0)
                sp.wait_ge(k_stored, 48 * (b + 1))
                for hp in range(2):
                    sp.dma_start(k2[par][HALF * hp:HALF * hp + HALF],
                                 stack_k[par].rearrange("(a hp) d c s -> hp (d c) a s", hp=2)[hp]).then_inc(k_ready, 16)

            def store_queries(par, half):
                cols = slice(2 * P * half, 2 * P * half + 2 * P)
                for i, pairs in enumerate(Q_ROWS):
                    for dst, src in ((stack_q, qp), (stack_qe, qe), (stack_qo, qo)):
                        sp.dma_start(dst[par].rearrange("h d c s -> (h d) c s")[:, pairs, cols],
                                     src[:, i:i + 1, cols].to_broadcast([P, len(range(NP)[pairs]), 2 * P])
                                     ).then_inc(q_stored[half], 16)

            def load_queries(b, par, g):
                sp.wait_ge(q_stored[g // 2], 144 * (b + 1))
                stands_alone(sp)
                at_least(sp, scored, 4 * UPG * (NC * b + g - 1))
                stands_alone(sp)
                q = slice(P * g, P * g + P)
                for hp in range(2):
                    rows = slice(HALF * hp, HALF * hp + HALF)
                    sp.dma_start(qh[rows, g % 2].rearrange("r (a hp) q -> r hp a q", hp=2)[:, hp],
                                 stack_q[par].rearrange("(a hp) d c s -> hp (d c) a s", hp=2)[hp][:, :, q]
                                 ).then_inc(q_ready[g % 2], 16)
                    sp.dma_start(qq[rows, g % 2],
                                 (stack_qe, stack_qo)[hp][par].rearrange("h d c s -> (d c) h s")[:, :, q]
                                 ).then_inc(q_ready[g % 2], 16)

            def store_out(b, back):
                G = NC * b - back
                if not live(G):
                    return
                at_least(sp, fin_made, G + 1)
                stands_alone(sp)
                bb, g = b - (back + NC - 1) // NC, (-back) % NC
                sp.dma_start(out_t[bb, g], out_sb[g % 2][:]).then_inc(out_stored[g % 2], 16)

            sp.wait_ge(x1_made, NC)
            sp.dma_start(x_in[:], x_t[1]).then_inc(x_loaded, 16)
            sp.wait_ge(zeroed, ZEROED)
            store_stacks(0, 0)
            load_queries(0, 0, 0)
            store_queries(0, 1)
            load_queries(0, 0, 1)

            def body(b, par, more):
                if more and not isinstance(b, int):
                    at_least(sp, x1_made, NC * (b + 1))
                    stands_alone(sp)
                    sp.dma_start(x_in[:], x_t[b + 1]).then_inc(x_loaded, 16)
                store_out(b, 3)
                load_queries(b, par, 2)
                store_out(b, 2)
                load_queries(b, par, 3)
                store_out(b, 1)
                if more:
                    store_stacks(b + 1, 1 - par)
                    load_queries(b + 1, 1 - par, 0)
                    store_queries(1 - par, 1)
                store_out(b, 0)
                if more:
                    load_queries(b + 1, 1 - par, 1)

            def tail(b):
                for back in (-1, -2, -3):
                    store_out(b, back)
                for i in range(2):
                    sp.wait_ge(out_stored[i], 16 * B * NC // 2)

            every_batch(sp, body, tail)

        @block.tensor
        def _(pe):
            def stage(b, k):
                n = NSTAGE * b + k
                m, part_k = divmod(k, 3)
                if k <= LAST_T and part_k == 0:
                    if m == 0:
                        at_least(pe, v_made, b)
                    else:
                        at_least(pe, xn_made[1], NC * b + m)
                    if m < NC:
                        at_least(pe, xn_made[0], NC * b + m + 1)
                else:
                    at_least(pe, pre_act, ACT_STAGES * b + by_act(k - 1))
                if k == VALUES:
                    for c in range(NC):
                        mm = pe.matmul(ps_a[:, P * c:P * c + P], xn2T[:, P * c:P * c + P], wv_sb[:],
                                       start=True, stop=True)
                elif k > LAST_T:
                    mm = pe.matmul(ps_a[:], (wk_sb if k == KEYS else wq_sb)[:], xn2T[:], start=True, stop=True)
                elif part_k == 0:
                    if m < NC:
                        mm = pe.transpose(ps_a[:, 0:P], xn1[:], ident)
                    if m > 0:
                        mm = pe.transpose(ps_a[:, P:2 * P], xn2[:], ident)
                elif part_k == UP:
                    for i in range(NC):
                        mm = pe.matmul(ps_a[:, P * i:P * i + P], w1_sb[:, P * i:P * i + P], xn1T[:],
                                       start=True, stop=True)
                else:
                    for i in range(NC):
                        mm = pe.matmul(ps_a[:, 0:D], hT[:, i, :], w2_sb[:, i, :], start=(i == 0), stop=(i == NC - 1))
                mm.then_inc(pre_mm, 1)

            def scores(b, par, t, chunks):
                g, j = divmod(t, UPG)
                u = UPB * b + t
                if t == 0 and 0 in chunks:
                    at_least(pe, k_ready, 32 * (b + 1))
                if j == 0 and 0 in chunks:
                    at_least(pe, q_ready[g % 2], 64 * (2 * b + g // 2 + 1))
                for c in chunks:
                    if c % 2 == 0:
                        at_least(pe, evacuated, 2 * u + c // 2 - 1)
                    bank = ps_s[:, COLS * c:COLS * c + COLS]
                    for a in range(H // 2):
                        pe.matmul(bank[:, 2 * UQ * a:2 * UQ * (a + 1)], k2[par][:, a, P * c:P * c + P],
                                  qh[:, g % 2, 2 * a:2 * a + 2, UQ * j:UQ * j + UQ],
                                  start=(a == 0), stop=False, skip_group_check=True)
                    if abs(c - g) <= 1:
                        cols = bank.rearrange("p (h q) -> p h q", h=H)
                        for q in range(0, UQ, 2):
                            j0 = P * (c - g) - UQ * j - q + TR0
                            mm = pe.matmul(cols[:, :, q:q + 2], tr[:, j0:j0 + P],
                                           qq[:, g % 2, :, UQ * j + q:UQ * j + q + 2],
                                           start=False, stop=(q == UQ - 2), skip_group_check=True)
                    else:
                        j0 = TRW - P if c > g else 0
                        mm = pe.matmul(bank, tr[:, j0:j0 + P], qq[:, g % 2, :, UQ * j:UQ * j + UQ],
                                       start=False, stop=True, skip_group_check=True)
                    mm.then_inc(scored, 1)

            def values(b, g, G, half):
                if half == 0:
                    at_least(pe, exped, UPG * (G + 1))
                    at_least(pe, o_copied, G)
                if g == 0:
                    at_least(pe, v_laid[half], 4 * b + 4)
                for c in range(2 * half, 2 * half + 2):
                    v = v_far if abs(c - g) > 1 else v_pad
                    for n, h in enumerate(BY_QUADRANT):
                        quad, _, region = seat(h)
                        mm = pe.matmul(ps_o[32 * quad:32 * quad + 32, P * region:P * region + P], v[:, c, h, :],
                                       w[g % 2][:, c, h, :], start=(c == 0 and n < 4), stop=False,
                                       skip_group_check=True)
                if half == 1:
                    mm.then_inc(v_used, 1)

            def compact(G):
                at_least(pe, o_copied, G + 1)
                at_least(pe, fin_made, G)
                for n, rows in enumerate((spread, gather)):
                    for region in range(2):
                        mm = pe.matmul(ps_b[:, P * n:P * n + P], rows[:, region, :], o_sb[:, region, :],
                                       start=(region == 0), stop=(region == 1))
                mm.then_inc(compacted, 1)

            def relative(g, G, half, ops=range(NO // 4)):
                for i in range(2):
                    at_least(pe, masked[i], 2 * G + half)
                at_least(pe, exped, UPG * G + 2 * (half + 1))
                for op in ops:
                    near = [c for c in range(NC) if abs(c - g) <= 1]
                    for c in near:
                        for jj in range(2):
                            oc = NO // 2 * half + 2 * op + jj
                            i0 = P * (c - g) - OCT * oc + TV0 - (OCT - 1)
                            mm = pe.matmul(ps_r[64 * jj:64 * jj + 64, P * op:P * op + P],
                                           tv[:, HD * i0:HD * (i0 + OCT)],
                                           w[g % 2][:, c, :, OCT * oc:OCT * oc + OCT],
                                           start=(c == near[0]), stop=(c == near[-1]))
                if ops[-1] == NO // 4 - 1:
                    mm.then_inc(rel_done, 1)

            def select(G):
                for i in range(2):
                    at_least(pe, masked[i], 2 * G + 2)
                for h in BY_QUADRANT:
                    quad, place, region = seat(h)
                    mm = pe.matmul(ps_o[32 * quad:32 * quad + 32, P * region:P * region + P], sel[:, place, :],
                                   rown[:, h, :], start=False, stop=(region == 1), skip_group_check=True)
                mm.then_inc(o_done, 1)

            def after(G, k):
                if k == 0:
                    at_least(pe, att_made, G + 1)
                    mm = pe.matmul(ps_b[:, 0:D], attT[:], wo_sb[:], start=True, stop=True)
                elif k == 1:
                    at_least(pe, xn_made[2], G + 1)
                    mm = pe.transpose(ps_b[:, 0:P], xn3[:], ident)
                elif k == 2:
                    at_least(pe, xn3T_made, G + 1)
                    for i in range(NC):
                        mm = pe.matmul(ps_b[:, P * i:P * i + P], w1_sb[:, P * i:P * i + P], xn3T[:],
                                       start=True, stop=True)
                else:
                    at_least(pe, h3_made, G + 1)
                    for i in range(NC):
                        mm = pe.matmul(ps_b[:, 0:D], h3T[:, i, :], w2_sb[:, i, :], start=(i == 0), stop=(i == NC - 1))
                mm.then_inc(post_mm, 1)

            def slot(b, par, t, more):
                g, j = divmod(t, UPG)
                G = NC * b + g
                first, middle, end = stages_at(t) if more else ((), (), ())
                vb, vg = (b - 1 if g == 0 else b), (g - 1) % NC
                if t < UPB:
                    scores(b, par, t, (0, 1))
                for k in first:
                    stage(b + 1, k)
                if j == 0 and live(G - 3):
                    after(G - 3, 1)
                if t < UPB:
                    scores(b, par, t, (2, 3))
                for k in middle:
                    stage(b + 1, k)
                if j == 0:
                    if live(G - 3):
                        after(G - 3, 2)
                    if live(G - 1):
                        relative(vg, G - 1, 0, range(0, 2))
                    if live(G - 2):
                        select(G - 2)
                    if live(G - 3):
                        after(G - 3, 3)
                elif j == 1:
                    if live(G - 1):
                        relative(vg, G - 1, 0, range(2, NO // 4))
                    if live(G - 2):
                        compact(G - 2)
                    if live(G - 1):
                        values(vb, vg, G - 1, 0)
                elif j == 2:
                    if live(G - 1):
                        values(vb, vg, G - 1, 1)
                    if live(G - 2):
                        after(G - 2, 0)
                else:
                    if live(G - 1):
                        relative(vg, G - 1, 1)
                for k in end:
                    stage(b + 1, k)

            pe.wait_ge(f_loaded, 16 * len(ffn_loads))
            for m in range(NC):
                pe.wait_ge(first_xn, m + 1)
                mm = pe.transpose(ps_a[:, P * m:P * m + P], xn4[0][:, m, :], ident)
            mm.then_inc(first_mm, 1)
            pe.wait_ge(first_act, 1)
            for i in range(NC):
                pe.matmul(ps_s[:, S * i:S * i + S], w1_sb[:, P * i:P * i + P], xn4T,
                          start=True, stop=True).then_inc(first_mm, 1)
            pe.wait_ge(first_act, 1 + NC)
            for m in range(NC):
                for i in range(NC):
                    mm = pe.matmul(ps_r[:, P * m:P * m + P], h4T[:, i, P * m:P * m + P], w2_sb[:, i, :],
                                   start=(i == 0), stop=(i == NC - 1))
            mm.then_inc(first_mm, 1)
            for m in range(NC):
                pe.wait_ge(first_xn, NC + m + 1)
                mm = pe.transpose(ps_a[:, P * m:P * m + P], xn4[1][:, m, :], ident)
            mm.then_inc(pre_mm, LAST_T + 1)
            pe.wait_ge(c_loaded, 16 * N_LOADS)
            for k in range(KEYS, NSTAGE):
                stage(0, k)
            pe.wait_ge(tr_step, 11)

            def body(b, par, more):
                for t in range(UPB):
                    slot(b, par, t, more)

            def tail(b):
                for t in range(UPB, UPB + TAIL):
                    slot(b, 1, t, False)

            every_batch(pe, body, tail)

        @block.scalar
        def _(act):
            def stage(b, k):
                if by_act(k) == by_act(k - 1):
                    return
                at_least(act, pre_mm, NSTAGE * b + k + 1)
                m, part_k = divmod(k, 3)
                if k == KEYS:
                    at_least(act, k_split, 3 * b)
                    at_least(act, k_stored, 48 * b)
                    act.activation(kf[:], ps_a[:], ACT.Identity, bias=bk_sb[:, 0:1])
                    ins = act.activation(kp[:, 0, :], ps_a[:], ACT.Identity, bias=bk_sb[:, 0:1])
                elif k == QUERIES:
                    at_least(act, q_split, 3 * b)
                    for i in range(2):
                        at_least(act, q_stored[i], 144 * b)
                    act.activation(qf[:], ps_a[:], ACT.Identity, bias=bq_sb[:, 0:1])
                    ins = act.activation(qp[:, 0, :], ps_a[:], ACT.Identity, bias=bq_sb[:, 0:1])
                elif part_k == 0:
                    if m < NC:
                        ins = act.copy(xn1T[:], ps_a[:, 0:P])
                    if m > 0:
                        ins = act.copy(xn2T[:, P * (m - 1):P * m], ps_a[:, P:2 * P])
                else:
                    for i in range(NC):
                        ins = act.activation(hT[:, i, :], ps_a[:, P * i:P * i + P], ACT.Relu, bias=b1_sb[:, i:i + 1])
                ins.then_inc(pre_act, 1)

            def evacuate(b, t, pair):
                g, j = divmod(t, UPG)
                u, G = UPB * b + t, NC * b + g
                if j == 0 and pair == 0:
                    at_least(act, rel_done, 2 * G - 2)
                at_least(act, scored, 4 * u + 2 * pair + 2)
                dst = w[g % 2][:, 2 * pair:2 * pair + 2, :, UQ * j:UQ * j + UQ].rearrange("p c h q -> p (c h) q")
                src = ps_s[:, 2 * COLS * pair:2 * COLS * (pair + 1)].rearrange("p (a q) -> p a q", q=UQ)
                act.copy(dst, src).then_inc(evacuated, 1)

            def exponent(u, t):
                g, j = divmod(t % UPB, UPG)
                at_least(act, shifted, u + 1)
                at_least(act, pool_shifted, u + 1)
                v = w[g % 2][:, :, :, UQ * j:UQ * j + UQ].rearrange("p c h q -> p (c h) q")
                act.activation(v, v, ACT.Exp, scale=SCALE).then_inc(exped, 1)

            def even_odd(b):
                at_least(act, q_split, 3 * b + 3)
                for i, dst in enumerate((qe, qo)):
                    ins = act.copy(dst[:].rearrange("p a (s two) -> p a s two", two=2)[:, :, :, i],
                                   qp[:].rearrange("p a (s two) -> p a s two", two=2)[:, :, :, i])
                ins.then_inc(qeo_made, 1)

            def slot(b, t, more):
                g, j = divmod(t, UPG)
                G = NC * b + g
                first, middle, end = stages_at(t) if more else ((), (), ())
                for k in first:
                    stage(b + 1, k)
                if j == 1 and live(G - 2):
                    at_least(act, o_done, G - 1)
                    act.copy(o_sb[:].rearrange("p r q -> p (r q)"), ps_o[:, 0:2 * P]).then_inc(o_copied, 1)
                if j == 0 and live(G - 3):
                    at_least(act, post_mm, 4 * (G - 3) + 2)
                    act.copy(xn3T[:], ps_b[:, 0:P]).then_inc(xn3T_made, 1)
                if t < UPB:
                    evacuate(b, t, 0)
                if j == 1 and t <= UPB + 1 and not (isinstance(b, int) and UPB * b + t < 2):
                    exponent(UPB * b + t - 2, t - 2)
                if t < UPB:
                    evacuate(b, t, 1)
                if more and t == QEO_SLOT:
                    even_odd(b + 1)
                for k in middle:
                    stage(b + 1, k)
                if j == 0 and live(G - 3):
                    at_least(act, post_mm, 4 * (G - 3) + 3)
                    for i in range(NC):
                        ins = act.activation(h3T[:, i, :], ps_b[:, P * i:P * i + P], ACT.Relu, bias=b1_sb[:, i:i + 1])
                    ins.then_inc(h3_made, 1)
                if t <= UPB + 1 and j != 1 and not (isinstance(b, int) and UPB * b + t < 2):
                    exponent(UPB * b + t - 2, t - 2)
                for k in end:
                    stage(b + 1, k)
                if t == V_SLOT:
                    lay_values(act, b, 1)

            act.wait_ge(zeroed, ZEROED)
            act.copy(warm[:], minus_half[:, 0:1])
            act.wait_ge(f_loaded, 16 * len(ffn_loads))
            act.wait_ge(first_mm, 1)
            act.copy(xn4T, ps_a[:]).then_inc(first_act, 1)
            for i in range(NC):
                act.wait_ge(first_mm, 2 + i)
                act.activation(h4T[:, i, :], ps_s[:, S * i:S * i + S], ACT.Relu,
                               bias=b1_sb[:, i:i + 1]).then_inc(first_act, 1)
            act.wait_ge(pre_mm, LAST_T + 1)
            act.copy(xn2T[:], ps_a[:]).then_inc(pre_act, by_act(LAST_T))
            act.wait_ge(c_loaded, 16 * N_LOADS)
            for k in range(KEYS, NSTAGE):
                stage(0, k)
            even_odd(0)

            def body(b, par, more):
                for t in range(UPB):
                    slot(b, t, more)

            def tail(b):
                for t in range(UPB, UPB + TAIL):
                    slot(b, t, False)

            every_batch(act, body, tail)

        @block.vector
        def _(dve):
            def normalise(i, src, dst):
                dve.tensor_scalar(dst, src, mv[:, i, 0:1], rstd[:, i:i + 1],
                                  ALU.subtract, ALU.mult).then_inc(xn_made[i], 1)

            def statistics(b, par, m, after):
                norms = []
                if m is not None and m < NC:
                    if m == 0:
                        at_least(dve, x_loaded, 16 * (b + 1))
                    norms.append((0, NC * b + m, x_in[:, m, :]))
                if m:
                    j, n = m - 1, NC * b + m - 1
                    at_least(dve, pre_mm, NSTAGE * b + 3 * j + 3)
                    if j == 0:
                        at_least(dve, xb_made, b + 1)
                    dve.scalar_tensor_tensor(out=x1[par][:, j, :], in0=ps_a[:, 0:D], scalar=0.5, in1=xb[:, j, :],
                                             op0=ALU.mult, op1=ALU.add).then_inc(x1_made, 1)
                    norms.append((1, n, x1[par][:, j, :]))
                if after:
                    G, g, after_par = after
                    at_least(dve, post_mm, 4 * G + 1)
                    at_least(dve, x1_biased, G + 1)
                    dve.tensor_tensor(x2[g % 2][:], ps_b[:, 0:D], x1[after_par][:, g, :], ALU.add).then_inc(x2_made, 1)
                    norms.append((2, G, x2[g % 2][:]))
                for i, n, src in norms:
                    if i > 0:
                        at_least(dve, (x1_made, x2_made)[i - 1], n + 1)
                    dve.bn_stats(st[:, i, :], src).then_inc(stats[i], 1)
                for i, n, _ in norms:
                    at_least(dve, stats[i], 2 * n + 1)
                    stands_alone(dve)
                    dve.bn_aggr(mv[:, i, :], st[:, i, :]).then_inc(stats[i], 1)
                for i, n, _ in norms:
                    at_least(dve, stats[i], 2 * n + 2)
                    if i == 1 or (i == 0 and m == 0):
                        dve.tensor_scalar(var[:, 0:2], mv[:, 0:2, 1], EPS, None, ALU.add).then_inc(var_made[0], 1)
                    elif i == 2:
                        dve.tensor_scalar(var[:, 2:3], mv[:, 2, 1:2], EPS, None, ALU.add).then_inc(var_made[1], 1)

            def norm_apply(b, par, m):
                at_least(dve, rstd_made[0], NORMS * b + m + 1)
                if m > 0:
                    normalise(1, x1[par][:, m - 1, :], xn2[:])
                if m < NC:
                    normalise(0, x_in[:, m, :], xn1[:])

            def stage(b, k):
                if k == QUERIES:
                    at_least(dve, pre_act, ACT_STAGES * b + by_act(k))
                    dve.tensor_tensor(qf[:], qf[:], qp[:, 0, :], ALU.subtract).then_inc(q_split, 1)
                    at_least(dve, q_split, 3 * b + 1)
                    dve.tensor_copy(qp[:, 1, :], qf[:]).then_inc(q_split, 1)
                    at_least(dve, q_split, 3 * b + 2)
                    dve.tensor_tensor(qp[:, 2, :], qf[:], qp[:, 1, :], ALU.subtract).then_inc(q_split, 1)
                elif k == VALUES:
                    at_least(dve, pre_mm, NSTAGE * b + k + 1)
                    at_least(dve, v_laid[0], 4 * b)
                    dve.tensor_tensor(v_raw[:], ps_a[:].rearrange("p (c d) -> p c d", c=NC),
                                      bv_sb[:].unsqueeze(1).to_broadcast([P, NC, D]), ALU.add).then_inc(v_made, 1)

            def chunk_max(b, t):
                g, j = divmod(t, UPG)
                u = UPB * b + t
                at_least(dve, evacuated, 2 * u + 2)
                v = w[g % 2][:, :, :, UQ * j:UQ * j + UQ]
                at_least(dve, maxed, u)
                dve.tensor_tensor(mtmp[:].rearrange("p c h q -> p (c h) q"),
                                  v[:, 0:2].rearrange("p c h q -> p (c h) q"),
                                  v[:, 2:4].rearrange("p c h q -> p (c h) q"), ALU.max).then_inc(mtmp_made, 1)
                at_least(dve, mtmp_made, u + 1)
                dve.tensor_tensor(mx[t % 2][:], mtmp[:, 0].rearrange("p h q -> p (h q)"),
                                  mtmp[:, 1].rearrange("p h q -> p (h q)"), ALU.max).then_inc(maxed, 1)

            def attention(G):
                at_least(dve, compacted, G + 1)
                dve.reciprocal(rden[:], ps_b[:, 0:P]).then_inc(rden_made, 1)
                at_least(dve, rden_made, G + 1)
                dve.tensor_tensor(attT[:], ps_b[:, P:2 * P], rden[:], ALU.mult).then_inc(att_made, 1)

            def finish(G, g, b_last):
                at_least(dve, post_mm, 4 * G + 4)
                at_least(dve, x2_biased, G + 1)
                at_least(dve, out_stored[g % 2], 16 * (2 * b_last + g // 2))
                dve.scalar_tensor_tensor(out=out_sb[g % 2][:], in0=ps_b[:, 0:D], scalar=0.5, in1=x2[g % 2][:],
                                         op0=ALU.mult, op1=ALU.add).then_inc(fin_made, 1)

            def slot(b, par, t, more):
                g, j = divmod(t, UPG)
                G = NC * b + g

                def back(n):
                    q, place = divmod(g - n, NC)
                    return place, (par + q) % 2, b + q

                norm = (t - 1) // 2 if more and t % 2 == 1 and t < 2 * NORMS else None
                if j == 0 and live(G - 2):
                    for jj in range(2):
                        mask(dve, G - 2, 1, jj)
                if j == 1 and live(G - 3):
                    place, _, bb = back(3)
                    finish(G - 3, place, bb)
                if j == 2 and live(G - 1):
                    for jj in range(2):
                        mask(dve, G - 1, 0, jj)
                if j == 2 and live(G - 2):
                    attention(G - 2)
                after = (G - 2, *back(2)[:2]) if j == 3 and live(G - 2) else None
                if norm is not None or after:
                    statistics(b + 1, 1 - par, norm, after)
                if more and t == Q_SLOT:
                    stage(b + 1, QUERIES)
                if more and t == V_RAW_SLOT:
                    stage(b + 1, VALUES)
                if t < UPB:
                    chunk_max(b, t)
                if norm is not None:
                    norm_apply(b + 1, 1 - par, norm)
                if j == 3 and live(G - 2):
                    at_least(dve, rstd_made[1], G - 1)
                    normalise(2, x2[back(2)[0] % 2][:], xn3[:])
                if t <= UPB and not (isinstance(b, int) and UPB * b + t == 0):
                    shift(dve, 0, UPB * b + t - 1, t - 1)

            dve.memset(qe[:], 0.0).then_inc(zeroed, 1)
            dve.memset(qo[:], 0.0).then_inc(zeroed, 1)
            dve.memset(mv[:], 1.0).then_inc(zeroed, 1)
            dve.wait_ge(f_loaded, 16 * len(ffn_loads))
            dve.tensor_scalar(b2_half[:], b2_sb[:], 0.5, None, ALU.mult).then_inc(half_made, 1)
            dve.wait_ge(zeroed, ZEROED)
            def first_norm(i, src):
                for m in range(NC):
                    dve.bn_stats(st4[:, m, :], src[:, m, :]).then_inc(first_stats, 1)
                for m in range(NC):
                    dve.wait_ge(first_stats, 2 * NC * i + m + 1)
                    dve.bn_aggr(mv4[:, m, :], st4[:, m, :]).then_inc(first_stats, 1)
                dve.wait_ge(first_stats, 2 * NC * (i + 1))
                dve.tensor_scalar(var4[:], mv4[:, :, 1], EPS, None, ALU.add).then_inc(first_var, 1)
                dve.wait_ge(first_root, i + 1)
                for m in range(NC):
                    dve.tensor_scalar(xn4[i][:, m, :], src[:, m, :], mv4[:, m, 0:1], rstd4[:, m:m + 1],
                                      ALU.subtract, ALU.mult).then_inc(first_xn, 1)

            dve.wait_ge(x_loaded, 16)
            first_norm(0, x_in)
            dve.wait_ge(first_mm, 2 + NC)
            dve.wait_ge(xb_made, 1)
            dve.scalar_tensor_tensor(out=x1[0][:], in0=ps_r[:].rearrange("p (m d) -> p m d", m=NC), scalar=0.5,
                                     in1=xb[:], op0=ALU.mult, op1=ALU.add).then_inc(x1_made, NC)
            dve.wait_ge(x1_made, NC)
            first_norm(1, x1[0])
            for s, n in ((stats[0], 2 * NC), (stats[1], 2 * NC), (var_made[0], NORMS),
                         (xn_made[0], NC), (xn_made[1], NC)):
                dve.sem_inc(s, n)
            dve.wait_ge(c_loaded, 16 * N_LOADS)
            split_keys(dve, 0)
            stage(0, QUERIES)
            stage(0, VALUES)
            for n in range(2):
                rows = slice(HALF * n, HALF * n + HALF)
                a, z = TR0 - REL + n, TR0 + REL + n
                dve.tensor_copy(trf[rows, 0:a], trf[rows, a:a + 1].to_broadcast([HALF, a])).then_inc(tr_step, 1)
                dve.tensor_copy(trf[rows, z + 1:TRW],
                                 trf[rows, z:z + 1].to_broadcast([HALF, TRW - z - 1])).then_inc(tr_step, 1)
            dve.wait_ge(tr_step, 4)
            dve.tensor_copy(trp, trf).then_inc(tr_step, 1)
            dve.wait_ge(tr_step, 5)
            dve.tensor_tensor(trr, trf, trp, ALU.subtract).then_inc(tr_step, 1)
            dve.wait_ge(tr_step, 6)
            dve.tensor_scalar(trf, trp, part[:, 0:1], None, ALU.mult).then_inc(tr_step, 1)
            dve.wait_ge(tr_step, 7)
            dve.tensor_copy(trp, trr).then_inc(tr_step, 1)
            dve.wait_ge(tr_step, 8)
            dve.tensor_tensor(trr, trr, trp, ALU.subtract).then_inc(tr_step, 1)
            dve.wait_ge(tr_step, 9)
            dve.scalar_tensor_tensor(out=trf, in0=trp, scalar=part[:, 1:2], in1=trf,
                                      op0=ALU.mult, op1=ALU.add).then_inc(tr_step, 1)
            dve.wait_ge(tr_step, 10)
            dve.scalar_tensor_tensor(out=tr[:], in0=trr, scalar=part[:, 2:3], in1=trf,
                                      op0=ALU.mult, op1=ALU.add).then_inc(tr_step, 1)

            def body(b, par, more):
                for t in range(UPB):
                    slot(b, par, t, more)

            def tail(b):
                for t in range(UPB, UPB + TAIL):
                    slot(b, 1, t, False)

            every_batch(dve, body, tail)

        @block.gpsimd
        def _(pool):
            def sum_values(b, n):
                at_least(pool, v_made, b + 1)
                at_least(pool, v_laid[1], 4 * b)
                src = v_raw[:, 2 * n:2 * n + 2, :].rearrange("p c (h d) -> p (c h) d", d=HD)
                dst = v_sum[:, 2 * n:2 * n + 2, :].rearrange("p c (h d) -> p (c h) d", d=HD)
                far = relv_far[:, n, :].unsqueeze(1).to_broadcast([P, 2 * H, HD])
                pool.tensor_tensor(dst, src, far, ALU.add).then_inc(v_sums, 1)

            def root(i, n):
                cols = (slice(0, 2), slice(2, 3))[i]
                at_least(pool, var_made[i], n + 1)
                pool.tensor_tensor(rstd[:, cols], var[:, cols], minus_half[:, 0:2 - i], ALU.pow).then_inc(rstd_made[i], 1)

            def bias_input(b):
                at_least(pool, x_loaded, 16 * (b + 1))
                at_least(pool, x1_made, NC * b)
                pool.tensor_tensor(xb[:], x_in[:], b2_half[:].unsqueeze(1).to_broadcast([P, NC, D]),
                                   ALU.add).then_inc(xb_made, 1)

            def bias_x1(b, par, j):
                at_least(pool, xn_made[1], NC * b + j + 1)
                pool.tensor_tensor(x1[par][:, j, :], x1[par][:, j, :], bo_sb[:], ALU.add).then_inc(x1_biased, 1)

            def bias_x2(G, g):
                at_least(pool, xn_made[2], G + 1)
                pool.tensor_tensor(x2[g % 2][:], x2[g % 2][:], b2_half[:], ALU.add).then_inc(x2_biased, 1)

            def slot(b, par, t, more):
                u = UPB * b + t
                g, j = divmod(t, UPG)
                G = NC * b + g
                if more and t % 2 == 1 and t < 2 * NORMS:
                    root(0, NORMS * (b + 1) + (t - 1) // 2)
                if j == 3 and live(G - 2):
                    root(1, G - 2)
                if t <= UPB and not (isinstance(b, int) and u == 0):
                    shift(pool, 1, u - 1, t - 1)
                if t < UPB:
                    at_least(pool, maxed, u + 1)
                    at_least(pool, shifted, u - 1)
                    at_least(pool, pool_shifted, u - 1)
                    stands_alone(pool)
                    pool.partition_all_reduce(mall[t % 2][:], mx[t % 2][:], P, RMAX).then_inc(max_known, 1)
                if more and t % 2 == 1 and 1 < t < 2 * NORMS:
                    bias_x1(b + 1, 1 - par, t // 2 - 1)
                if j == 3 and live(G - 2):
                    bias_x2(G - 2, (g - 2) % NC)
                if more and t == 1:
                    bias_input(b + 1)
                if t == V_SLOT:
                    lay_values(pool, b, 0)
                if t == 0:
                    for n in range(2):
                        sum_values(b, n)
                if more and t == K_SLOT:
                    split_keys(pool, b + 1)

            pool.memset(minus_half[:], -0.5).then_inc(zeroed, 1)
            pool.memset(qh[:], 0.0).then_inc(zeroed, 1)
            pool.memset(v_pad[:], 0.0).then_inc(ones_set, 1)
            pool.memset(v_far[:], 0.0).then_inc(ones_set, 1)
            pool.wait_ge(ones_set, 2)
            for dst in (v_pad, v_far):
                for place in range(4):
                    lo, hi, step = (place, 12, 3) if place < 3 else (12, H, 1)
                    c1 = SUM_ROW + place % 3
                    ins = pool.memset(dst[:, :, lo:hi:step, c1:c1 + 1], 1.0)
                ins.then_inc(zeroed, 1)
            pool.wait_ge(zeroed, ZEROED)
            pool.wait_ge(f_loaded, 16 * len(ffn_loads))
            pool.wait_ge(half_made, 1)
            bias_input(0)
            for i in range(2):
                pool.wait_ge(first_var, i + 1)
                pool.tensor_tensor(rstd4[:], var4[:], minus_half[:], ALU.pow).then_inc(first_root, 1)
            pool.sem_inc(rstd_made[0], NORMS)
            pool.wait_ge(first_xn, 2 * NC)
            pool.tensor_tensor(x1[0][:], x1[0][:], bo_sb[:].unsqueeze(1).to_broadcast([P, NC, D]),
                               ALU.add).then_inc(x1_biased, NC)
            pool.wait_ge(c_loaded, 16 * N_LOADS)

            def body(b, par, more):
                for t in range(UPB):
                    slot(b, par, t, more)

            def tail(b):
                for t in range(UPB, UPB + TAIL):
                    slot(b, 1, t, False)

            every_batch(pool, body, tail)


def kernel(**inputs):
    import concourse.bacc as bacc
    from concourse.bass_utils import run_bass_kernel_spmd

    a = {k.removeprefix("L0_"): np.asarray(v) for k, v in inputs.items()}

    def rows(v):
        return np.broadcast_to(v, (P, v.shape[0]))

    arrays = {
        "x": a["attn_x"],
        "wqT": a["attn_Wq"].T, "wkT": a["attn_Wk"].T, "wvT": a["attn_Wv"].T, "woT": a["attn_Wo"].T,
        "bq": a["attn_bq"].reshape(P, 1), "bk": a["attn_bk"].reshape(P, 1),
        "bv": rows(a["attn_bv"]), "bo": rows(a["attn_bo"]),
        "relkT": a["attn_rel_k"].T, "relv": a["attn_rel_v"],
        "w1": a["ffn_W1"], "b1": a["ffn_b1"].reshape(NC, P).T, "w2": a["ffn_W2"], "b2": rows(a["ffn_b2"]),
        "cst": constants(),
    }
    arrays = {k: np.ascontiguousarray(v) for k, v in arrays.items()}
    nc = bacc.Bacc("TRN2", target_bir_lowering=False, num_devices=1)
    args = [nc.dram_tensor(k, v.shape, mybir.dt.from_np(v.dtype), kind="ExternalInput").ap()
            for k, v in arrays.items()]
    out = nc.dram_tensor("out", (B, S, D), F32, kind="ExternalOutput").ap()
    build(nc, *args, out)
    r = run_bass_kernel_spmd(nc, [arrays], core_ids=[0])
    return r.results[0]["out"]
```
